# Optimizing a Trainium2 kernel written in Bass

```python
import numpy as np
import jax
import jax.numpy as jnp

def _softmax(x, axis=-1):
    return jax.nn.softmax(x, axis=axis)

def _gelu(x):
    return jax.nn.gelu(x, approximate=True)

def _silu(x):
    return jax.nn.silu(x)

def _sigmoid(x):
    return jax.nn.sigmoid(x)

def _layernorm(x, axis=-1, eps=1e-05):
    m = jnp.mean(x, axis=axis, keepdims=True)
    v = jnp.var(x, axis=axis, keepdims=True)
    return (x - m) / jnp.sqrt(v + eps)

def _scatter_add(tgt, idx, src, axis=0):
    return tgt.at[idx].add(src)

def _segment_sum(src, seg, n):
    return jax.ops.segment_sum(src, seg, n)
kernel_name = 'mk_gnn_preln_d2_gnn_r64_0b1a18'

def setup_inputs(seed: int=0):
    np.random.seed(seed)
    _w = jnp.asarray

    def _rec_inputs():
        import jax
        import jax.numpy as jnp
        _gk = jax.random.key(seed)
        x = -0.000202 + 1 * jax.random.normal(jax.random.fold_in(_gk, 1), (50000, 128), jnp.float32)
        src = jax.random.randint(jax.random.fold_in(_gk, 2), (12500,), 0, 50000, jnp.int32)
        dst = jax.random.randint(jax.random.fold_in(_gk, 3), (12500,), 0, 50000, jnp.int32)
        _o = jnp.argsort(dst, stable=True)
        src = src[_o]
        dst = dst[_o]
        edge_attr_128 = 5.93493e-05 + 1.00006 * jax.random.normal(jax.random.fold_in(_gk, 13), (12500, 128), jnp.float32)
        edge_weight = jax.random.uniform(jax.random.fold_in(_gk, 15), (12500,), jnp.float32, 0.0, 0.999999)
        return (x, src, dst, edge_attr_128, edge_weight)
    x, src, dst, edge_attr_128, edge_weight = _rec_inputs()

    def _L0_gnn_setup():
        import jax, jax.numpy as jnp
        import numpy as np
        N_NODES = 50000
        N_EDGES = 625000
        IN_DIM = 128
        OUT_DIM = 128
        NEG_SLOPE = 0.01
        key = jax.random.key(seed)
        ks = jax.random.split(key, 8)
        return {'entity_embed': jax.random.normal(ks[0], (N_NODES, IN_DIM), dtype=jnp.float32), 'out_sqrt_degree': jax.random.uniform(ks[1], (N_NODES, 1), dtype=jnp.float32), 'in_sqrt_degree': jax.random.uniform(ks[2], (N_NODES, 1), dtype=jnp.float32), 'edge_src': jax.random.randint(ks[3], (N_EDGES,), 0, N_NODES, dtype=jnp.int32), 'edge_dst': jax.random.randint(ks[4], (N_EDGES,), 0, N_NODES, dtype=jnp.int32), 'edge_weight': jax.random.uniform(ks[5], (N_EDGES,), dtype=jnp.float32), 'W_weight': jax.random.normal(ks[6], (OUT_DIM, IN_DIM), dtype=jnp.float32) / np.sqrt(IN_DIM), 'W_bias': jnp.zeros((OUT_DIM,), dtype=jnp.float32)}
    _L0_gnn_all = _L0_gnn_setup()
    _L0_gnn_in = {k: v for k, v in _L0_gnn_all.items() if k in ('W_weight', 'W_bias')}
    del _L0_gnn_all

    def _L1_gnn_setup():
        import jax, jax.numpy as jnp
        import numpy as np
        N = 50000
        E = 9375
        D = 128
        L = 4
        NEG_SLOPE = 0.2
        LN_EPS = 1e-05

        def _segment_softmax(logits, dst, num_segments):
            m = jax.ops.segment_max(logits, dst, num_segments=num_segments)
            m = jnp.where(jnp.isfinite(m), m, 0.0)
            ex = jnp.exp(logits - m[dst])
            denom = jax.ops.segment_sum(ex, dst, num_segments=num_segments)
            return ex / (denom[dst] + 1e-16)

        def _gat_layer(x, src, dst, ea, W, We, a_s, a_d, a_e, b, g, beta):
            h = x @ W
            e = ea @ We
            alpha = h @ a_s
            alpha = alpha[src] + (h @ a_d)[dst] + e @ a_e
            alpha = jax.nn.leaky_relu(alpha, NEG_SLOPE)
            alpha = _segment_softmax(alpha, dst, N)
            out = jax.ops.segment_sum(h[src] * alpha[:, None], dst, num_segments=N) + b
            mu = out.mean(-1, keepdims=True)
            var = ((out - mu) ** 2).mean(-1, keepdims=True)
            return (out - mu) * jax.lax.rsqrt(var + LN_EPS) * g + beta
        key = jax.random.key(seed)
        ks = jax.random.split(key, 12)
        inp = {'x': jax.random.normal(ks[0], (N, D), dtype=jnp.float32), 'edge_index': jax.random.randint(ks[1], (2, E), 0, N, dtype=jnp.int64), 'edge_attr': jax.random.normal(ks[2], (E, D), dtype=jnp.float32)}
        s = 1.0 / np.sqrt(D)
        inp['W'] = jax.random.normal(ks[3], (L, D, D), dtype=jnp.float32) * s
        inp['We'] = jax.random.normal(ks[4], (L, D, D), dtype=jnp.float32) * s
        inp['att_src'] = jax.random.normal(ks[5], (L, D), dtype=jnp.float32) * s
        inp['att_dst'] = jax.random.normal(ks[6], (L, D), dtype=jnp.float32) * s
        inp['att_edge'] = jax.random.normal(ks[7], (L, D), dtype=jnp.float32) * s
        inp['bias'] = jnp.zeros((L, D), dtype=jnp.float32)
        inp['ln_gamma'] = jnp.ones((L, D), dtype=jnp.float32)
        inp['ln_beta'] = jnp.zeros((L, D), dtype=jnp.float32)
        return inp
    _L1_gnn_all = _L1_gnn_setup()
    _L1_gnn_in = {k: v for k, v in _L1_gnn_all.items() if k in ('W', 'We', 'att_src', 'att_dst', 'att_edge', 'bias', 'ln_gamma', 'ln_beta')}
    del _L1_gnn_all
    return {'x': x, 'src': src, 'dst': dst, 'edge_attr_128': edge_attr_128, 'edge_weight': edge_weight, 'L0_gnn_W_weight': _L0_gnn_in['W_weight'], 'L0_gnn_W_bias': _L0_gnn_in['W_bias'], 'L1_gnn_W': _L1_gnn_in['W'], 'L1_gnn_We': _L1_gnn_in['We'], 'L1_gnn_att_src': _L1_gnn_in['att_src'], 'L1_gnn_att_dst': _L1_gnn_in['att_dst'], 'L1_gnn_att_edge': _L1_gnn_in['att_edge'], 'L1_gnn_bias': _L1_gnn_in['bias'], 'L1_gnn_ln_gamma': _L1_gnn_in['ln_gamma'], 'L1_gnn_ln_beta': _L1_gnn_in['ln_beta']}

def reference(x, src, dst, edge_attr_128, edge_weight, L0_gnn_W_weight, L0_gnn_W_bias, L1_gnn_W, L1_gnn_We, L1_gnn_att_src, L1_gnn_att_dst, L1_gnn_att_edge, L1_gnn_bias, L1_gnn_ln_gamma, L1_gnn_ln_beta):
    import jax
    import jax.numpy as jnp

    def _L0_gnn_ref(entity_embed, out_sqrt_degree, in_sqrt_degree, edge_src, edge_dst, edge_weight, W_weight, W_bias):
        import jax, jax.numpy as jnp
        import numpy as np
        N_NODES = 50000
        N_EDGES = 625000
        IN_DIM = 128
        OUT_DIM = 128
        NEG_SLOPE = 0.01
        node = entity_embed * out_sqrt_degree
        msg = node[edge_src] * edge_weight[:, None]
        N_h = jax.ops.segment_sum(msg, edge_dst, num_segments=N_NODES)
        N_h = N_h * in_sqrt_degree
        out = (entity_embed + N_h) @ W_weight.T + W_bias
        return jnp.where(out >= 0, out, NEG_SLOPE * out)

    def _L1_gnn_ref(x, edge_index, edge_attr, W, We, att_src, att_dst, att_edge, bias, ln_gamma, ln_beta):
        import jax, jax.numpy as jnp
        import numpy as np
        N = 50000
        E = 9375
        D = 128
        L = 4
        NEG_SLOPE = 0.2
        LN_EPS = 1e-05

        def _segment_softmax(logits, dst, num_segments):
            m = jax.ops.segment_max(logits, dst, num_segments=num_segments)
            m = jnp.where(jnp.isfinite(m), m, 0.0)
            ex = jnp.exp(logits - m[dst])
            denom = jax.ops.segment_sum(ex, dst, num_segments=num_segments)
            return ex / (denom[dst] + 1e-16)

        def _gat_layer(x, src, dst, ea, W, We, a_s, a_d, a_e, b, g, beta):
            h = x @ W
            e = ea @ We
            alpha = h @ a_s
            alpha = alpha[src] + (h @ a_d)[dst] + e @ a_e
            alpha = jax.nn.leaky_relu(alpha, NEG_SLOPE)
            alpha = _segment_softmax(alpha, dst, N)
            out = jax.ops.segment_sum(h[src] * alpha[:, None], dst, num_segments=N) + b
            mu = out.mean(-1, keepdims=True)
            var = ((out - mu) ** 2).mean(-1, keepdims=True)
            return (out - mu) * jax.lax.rsqrt(var + LN_EPS) * g + beta
        src, dst = (edge_index[0], edge_index[1])
        esum = jax.ops.segment_sum(edge_attr, dst, num_segments=N)
        cnt = jax.ops.segment_sum(jnp.ones((src.shape[0],), edge_attr.dtype), dst, num_segments=N)
        loop_attr = esum / jnp.maximum(cnt, 1.0)[:, None]
        loop = jnp.arange(N, dtype=src.dtype)
        src_f = jnp.concatenate([src, loop])
        dst_f = jnp.concatenate([dst, loop])
        ea_f = jnp.concatenate([edge_attr, loop_attr], axis=0)
        for l in range(L):
            x = _gat_layer(x, src_f, dst_f, ea_f, W[l], We[l], att_src[l], att_dst[l], att_edge[l], bias[l], ln_gamma[l], ln_beta[l])
        return x
    edge_index = jnp.stack([src, dst])
    deg = jnp.maximum(jax.ops.segment_sum(jnp.ones(dst.shape, jnp.float32), dst, num_segments=50000), 1.0)
    deg_isqrt = deg ** (-0.5)
    h = jnp.maximum(_layernorm(x, axis=-1), 0.0)
    x = x + _L0_gnn_ref(h, deg_isqrt[:, None], deg_isqrt[:, None], src, dst, edge_weight, L0_gnn_W_weight, L0_gnn_W_bias)
    h = jnp.maximum(_layernorm(x, axis=-1), 0.0)
    x = x + _L1_gnn_ref(h, edge_index, edge_attr_128, L1_gnn_W, L1_gnn_We, L1_gnn_att_src, L1_gnn_att_dst, L1_gnn_att_edge, L1_gnn_bias, L1_gnn_ln_gamma, L1_gnn_ln_beta)
    return x

_drawn_inputs = setup_inputs


def setup_inputs(seed=0):
    import zlib

    import numpy as np

    out = dict(_drawn_inputs(seed))
    spreads = {'L0_gnn_W_bias': (0.0, 0.1),
     'L1_gnn_bias': (0.0, 0.1),
     'L1_gnn_ln_gamma': (1.0, 0.2),
     'L1_gnn_ln_beta': (0.0, 0.1)}
    factors = {'edge_attr_128': 3.29,
     'L1_gnn_We': 3.305,
     'L1_gnn_att_dst': 150.45,
     'L1_gnn_att_edge': 3.106,
     'L1_gnn_att_src': 2.979}
    for name, (base, spread) in spreads.items():
        noise = np.random.default_rng([zlib.crc32(name.encode()), seed]).standard_normal(out[name].shape)
        drawn = base * np.exp(spread * noise) if base else spread * noise
        out[name] = jnp.asarray(drawn.astype(out[name].dtype))
    for name, factor in factors.items():
        out[name] = (out[name] * factor).astype(out[name].dtype)
    return out
```

```python
import concourse.bass as bass
from concourse import mybir
from contextlib import ExitStack

F32 = mybir.dt.float32
I32 = mybir.dt.int32
BF16 = mybir.dt.bfloat16
ALU = mybir.AluOpType
ACT = mybir.ActivationFunctionType
AX = mybir.AxisListType

D = 128
N = 50000
E = 12500
L = 4
P = 125
C = E // P
Q = 4
NS = 4
ROUND = P * NS * Q
ROUNDS = N // ROUND
CORE = 112
EPS = 1e-5
BIG = 1e30
NOWHERE = 1 << 23
SHARES = [10, 4, 4, 4, 3]


def gnn_kernel(nc, x, src, dst, ea, ew, w0, b0, wg, we, att_s, att_d, att_e, bg, gamma, beta, out):
    ctx = ExitStack()
    with ctx:
        ctx.enter_context(nc.allow_non_contiguous_dma(reason="a few hundred single elements, once"))

        def sb(name, shape, dt=F32):
            return ctx.enter_context(nc.sbuf_tensor(name, shape, dt))

        def sem(name):
            return ctx.enter_context(nc.semaphore(name))

        class Signal:

            def __init__(self, name):
                self.s, self.base = sem(name), 0

            def at(self, n):
                return self.s, self.base + n

        signals = {}

        def signal(*names):
            for n in names:
                if n not in signals:
                    signals[n] = Signal(n)
            got = [signals[n] for n in names]
            return got if len(got) > 1 else got[0]

        S = sb("S", [P, C, D])
        T = sb("T", [P, C, D])
        R = sb("R", [P, C + 1, D])
        X = sb("X", [P, 2, NS * Q, D])
        YB = sb("Y", [D, NS, Q, D])
        Y = YB[0:P, :, :, :]
        XT = sb("XT", [D, NS, Q * P])
        ident = sb("ident", [D, D])
        ones = sb("ones", [D, D])
        ones3 = sb("ones3", [3, D], BF16)
        W0 = sb("W0", [D, D])
        WC = sb("WC", [D, L, D])
        SD = sb("SD", [D, L, 2])
        VE = sb("VE", [D, L])
        BR = sb("BR", [3, L + 1, D], BF16)
        GC = sb("GC", [D, L])
        BC = sb("BC", [D, L])
        G3 = sb("G3", [P, D])
        B3 = sb("B3", [P, D])
        B0 = sb("B0", [P, D])
        MF = sb("MF", [P, P])
        MB = sb("MB", [P, P])
        PM = sb("PM", [P, P])
        DG = sb("DG", [P, P])
        CAR = sb("CAR", [P, D])

        def cols(name, dt=F32):
            return sb(name, [P, C], dt)

        keep, knext, rep, first, last, pen, penf = (cols(n) for n in (
            "keep", "knext", "rep", "first", "last", "pen", "penf"))
        srcI, dstI, repI = (cols(n, I32) for n in ("srcI", "dstI", "repI"))
        wE, lg, ls, run, mx, tmp, alpha, aself, isq = (cols(n) for n in (
            "wE", "lg", "ls", "run", "mx", "tmp", "alpha", "aself", "isq"))
        AE = sb("AE", [P, C, L])
        AL = sb("AL", [P, C, L])
        INFO = sb("INFO", [P, C, 2])
        INFG = sb("INFG", [P, C, 2])
        SCS = sb("SCS", [P, C, 2])
        SCT = sb("SCT", [P, C, 2])
        st = sb("st", [P, 2, Q, 6])
        mv = sb("mv", [P, NS, Q, 2])
        rt = sb("rt", [P, NS, Q])
        epsc = sb("epsc", [P, 1])
        taken = sb("taken", [P, 2])
        rr = sb("rr", [P, NS, Q])
        ss = sb("ss", [P, NS, Q])
        car1 = sb("car1", [P, L])

        PT = [ctx.enter_context(nc.psum_tensor(f"PT{s}", [D, 512], F32)) for s in range(NS)]
        PZ = [ctx.enter_context(nc.psum_tensor(f"PZ{s}", [D, Q, D], F32)) for s in range(NS)]

        info_t = nc.dram_tensor("info_t", [N, 2], F32, kind="Internal").ap()
        row_t = nc.dram_tensor("row_t", [E, D], F32, kind="Internal").ap()
        x1_t = nc.dram_tensor("x1_t", [E, D], F32, kind="Internal").ap()
        row_v = row_t.rearrange("(p c) f -> p c f", p=P)
        x1_v = x1_t.rearrange("(p c) f -> p c f", p=P)
        x_v = x.rearrange("(i p r) f -> i p r f", p=P, r=NS * Q)
        out_v = out.rearrange("(i p r) f -> i p r f", p=P, r=NS * Q)

        def dma2(eng, dst_ap, src_ap, s):
            eng.dma_start(dst_ap[0:CORE], src_ap[0:CORE]).then_inc(s, 16)
            eng.dma_start(dst_ap[CORE:P], src_ap[CORE:P]).then_inc(s, 16)

        class Chain:

            def __init__(self, dve, name, per=0):
                self.dve, self.done, self.per, self.n, self.base = dve, signal(name), per, 0, 0

            def turn(self, i):
                self.base, self.n = i * self.per, 0

            def add(self, ins):
                ins.then_inc(self.done.s, 1)
                self.n += 1

            def wait(self):
                self.dve.wait_ge(*self.done.at(self.base + self.n))

            def link(self, ins):
                self.add(ins)
                self.wait()

            def end(self, total=None):
                self.done.base += self.base + self.n if total is None else total

        def take_wait(n):
            nc.vector.memset(taken[:, n:n + 1], 0.0)

        def row_stats(ch, src4, s, ready):
            take_wait(0)
            for a in range(Q):
                ch.add(nc.vector.bn_stats(st[:, s % 2, a, :], src4[:, a, :]))
            ch.wait()
            take_wait(1)
            for a in range(Q):
                ins = nc.vector.bn_aggr(mv[:, s, a, :], st[:, s % 2, a, :])
            ins.then_inc(ready, 1)

        def row_normal(ch, src4, dst4, s, ready):
            ch.link(nc.vector.reciprocal(rr[:, s, :], rt[:, s, :]))
            for a in range(Q):
                ins = nc.vector.tensor_scalar(dst4[:, a, :], src4[:, a, :], mv[:, s, a, 0:1],
                                              rr[:, s, a:a + 1], ALU.subtract, ALU.mult)
            ins.then_inc(ready, 1)

        LN_LINKS = Q + 1

        def leaky(o, v, slope):
            return nc.vector.scalar_tensor_tensor(o, v, slope, v, ALU.mult, ALU.max)

        def roots(v, s):
            return nc.scalar.activation(rt[:, s, :], v, ACT.Sqrt, bias=epsc[:, 0:1])

        def wide(v, n=Q):
            return v.unsqueeze(2).broadcast_to([P, n, D])

        def transposes(ps, tiles):
            for a, t in enumerate(tiles):
                ins = nc.tensor.transpose(ps[:, a * P:(a + 1) * P], t, ident[0:P, 0:P])
            return ins

        def products(pz, xt, w, bias):
            if bias is not None:
                nc.tensor.matmul(pz[0:P, :, :], ones3[:, 0:P],
                                 BR[:, bias:bias + 1, :].broadcast_to([3, Q, D]),
                                 start=True, stop=False, skip_group_check=True)
            for a in range(Q):
                ins = nc.tensor.matmul(pz[0:P, a, :], xt[:, a * P:(a + 1) * P], w,
                                       start=bias is None and a == 0, stop=True, skip_group_check=True)
            return ins

        def gather(pool, to, idx, table, rows, done):
            pool.indirect_dma_start(to, None, table, bass.IndirectOffsetOnAxis(ap=idx, axis=0),
                                    bounds_check=rows - 1, oob_is_err=False).then_inc(done, 16)

        def scatter(pool, table, idx, rows, frm, done):
            pool.indirect_dma_start(table, bass.IndirectOffsetOnAxis(ap=idx, axis=0), frm, None,
                                    bounds_check=rows - 1, oob_is_err=False).then_inc(done, 16)

        def gather_x(pool, to, idx, c0, c1, done):
            for c in range(c0, c1):
                gather(pool, to[:, c, :], idx[:, c:c + 1], x, N, done)

        def pairs(eng, n, turn):
            if n >= 4:
                with eng.Fori(0, n // 2) as ii:
                    turn(ii * 2, 0)
                    turn(ii * 2 + 1, 1)
                rest = n // 2 * 2
            else:
                rest = 0
            for i in range(rest, n):
                turn(i, i % 2)

        s_w = sem("weights_loaded")
        s_meta = sem("edges_loaded")
        s_halo = sem("halo_cleared")
        s_id = sem("identity_ready")
        s_bs = sem("bias_split")
        s_br = sem("bias_rows_placed")
        s_wT = sem("w0_transposed")
        s_diag = sem("diagonal_ready")
        s_bc = sem("row_broadcast")
        s_ea = sem("edge_attr_loaded")
        s_fill = sem("info_filled")
        s_filled = sem("info_table_filled")
        s_idx = sem("indices_loaded")
        s_xsrc = sem("x_src_gathered")
        s_xdst = sem("x_dst_gathered")

        wide0 = XT[:, :, :].rearrange("p s q -> p (s q)")
        WR = wide0[:, 0:L * D].rearrange("p (l f) -> p l f", l=L)
        WER = wide0[:, 512:512 + L * D].rearrange("p (l f) -> p l f", l=L)
        PR = wide0[:, 1024:1024 + L * D].rearrange("p (l f) -> p l f", l=L)
        W0R = wide0[:, 1536:1536 + D]
        rowm = wide0[:, 1664:1664 + L]
        Yb = YB[:, :, :, :].rearrange("p s q f -> p (s q f)")
        attb = Yb[:, 1408:1408 + L * D]
        Yf = Yb[0:P]
        DH = Yf[:, 0:C + 2].bitcast(I32)
        DF = Yf[:, 128:128 + C + 2]
        brow = Yf[0:1, 256:256 + (L + 1) * D].rearrange("p (l f) -> p l f", l=L + 1)
        blo = X[0:1, 1, 8:13, :]
        bm = Yf[0:1, 1000:1000 + L + 1]
        bpart = X[0:1, 1, 0:8, :].rearrange("p a f -> p (a f)")[:, 0:960].bitcast(BF16) \
            .rearrange("p (k l f) -> p k l f", k=3, l=L + 1)
        fill = X[:, 0, :, :].rearrange("p a f -> p (a f)")[:, 0:800].rearrange("p (n k) -> p n k", k=2)

        with nc.Block() as block:
            @block.sync
            def _(sp):
                for a, b in ((WR, wg.rearrange("l k j -> k l j")), (WER, we.rearrange("l k j -> k l j")),
                             (W0R, w0), (GC[:, :], gamma.rearrange("l f -> f l")),
                             (BC[:, :], beta.rearrange("l f -> f l")),
                             (brow[:, 0:L, :], bg.unsqueeze(0)), (brow[:, L, :], b0.unsqueeze(0)),
                             (G3[:, :], gamma[L - 1:L, :].broadcast_to([P, D])),
                             (B3[:, :], beta[L - 1:L, :].broadcast_to([P, D])),
                             (B0[:, :], b0.unsqueeze(0).broadcast_to([P, D]))):
                    sp.dma_start(a, b).then_inc(s_w, 16)
                dv = dst.rearrange("(p c) -> p c", p=P)
                sp.wait_ge(s_halo, 1)
                sp.dma_start(DH[:, 1:C + 1], dv).then_inc(s_meta, 16)
                sp.dma_start(DH[1:P, 0:1], dv[0:P - 1, C - 1:C]).then_inc(s_meta, 16)
                sp.dma_start(DH[0:P - 1, C + 1:C + 2], dv[1:P, 0:1]).then_inc(s_meta, 16)
                sp.dma_start(wE[:, :], ew.rearrange("(p c) -> p c", p=P)).then_inc(s_meta, 16)
                sp.wait_ge(s_bs, 1)
                for k in range(3):
                    sp.dma_start(BR[k:k + 1, :, :], bpart[:, k, :, :]).then_inc(s_br, 16)
                sp.wait_ge(s_br, 48)
                sp.wait_ge(s_fill, 1)
                dma2(sp, info_t.rearrange("(p n) k -> p n k", p=P), fill, s_filled)
                dma2(sp, R[:, 1:C + 1, :], ea.rearrange("(p c) f -> p c f", p=P), s_ea)
                sp.dma_start(srcI[:, :], src.rearrange("(p c) -> p c", p=P)).then_inc(s_idx, 16)
                sp.dma_start(dstI[:, :], dv).then_inc(s_idx, 16)
                sp.wait_ge(s_filled, 32)
                sp.wait_ge(s_idx, 32)

            s_att = sem("att_loaded")
            s_attf = sem("att_used")

            @block.scalar
            def _(act):
                for n, att in enumerate((att_s, att_d, att_e)):
                    if n:
                        act.wait_ge(s_attf, n)
                    act.dma_start(attb[:, :], att.rearrange("l f -> (l f)").unsqueeze(0)
                                  .broadcast_to([D, L * D])).then_inc(s_att, 16)
                act.wait_ge(s_att, 48)

            @block.gpsimd
            def _(pool):
                z1 = sem("zeros_set")
                nc.gpsimd.memset(ident[:, :], 0.0).then_inc(z1, 1)
                nc.gpsimd.memset(ones[:, :], 1.0)
                nc.gpsimd.memset(ones3[:, :], 1.0)
                nc.gpsimd.memset(epsc[:, :], EPS)
                nc.gpsimd.memset(MF[:, :], 1.0).then_inc(z1, 1)
                nc.gpsimd.memset(MB[:, :], 1.0).then_inc(z1, 1)
                pool.wait_ge(z1, 3)
                nc.gpsimd.affine_select(out=ident[:, :], in_=ident[:, :], compare_op=ALU.not_equal,
                                        fill=1.0, base=0, pattern=[[-1, D]], channel_multiplier=1)
                nc.gpsimd.affine_select(out=MF[:, :], in_=MF[:, :], compare_op=ALU.is_gt, fill=0.0,
                                        base=0, pattern=[[1, P]], channel_multiplier=-1)
                nc.gpsimd.affine_select(out=MB[:, :], in_=MB[:, :], compare_op=ALU.is_gt, fill=0.0,
                                        base=0, pattern=[[-1, P]], channel_multiplier=1)
                nc.gpsimd.iota(INFO[:, :, 0].bitcast(I32), pattern=[[1, C]], base=0,
                               channel_multiplier=C).then_inc(s_id, 1)

            @block.tensor
            def _(pe):
                pe.wait_ge(s_id, 1)
                pe.wait_ge(s_w, 160)
                nc.tensor.transpose(PT[0][:, 0:D], W0R, ident[:, :]).then_inc(s_wT, 1)
                for n in range(2):
                    pe.wait_ge(s_diag, n + 1)
                    nc.tensor.matmul(PZ[n][0:P, 0, 0:P], ones[0:P, 0:P], DG[:, :],
                                     start=True, stop=True).then_inc(s_bc, 1)

            @block.vector
            def _(dve):
                ch = Chain(dve, "setup_chain")
                ch.add(nc.vector.memset(R[:, 0, :], 0.0))
                ch.add(nc.vector.memset(DH[:, :], NOWHERE))
                ch.wait()
                nc.vector.memset(fill[:, :, 0].bitcast(I32), NOWHERE).then_inc(s_halo, 1)
                nc.vector.memset(fill[:, :, 1], 1.0).then_inc(s_fill, 1)
                dve.wait_ge(s_w, 160)
                dve.wait_ge(s_wT, 1)
                ch.link(nc.vector.tensor_copy(W0[:, :], PT[0][:, 0:D]))
                ch.link(nc.vector.tensor_reduce(rowm, WR, AX.X, ALU.add))
                ch.link(nc.vector.tensor_scalar(rowm, rowm, 1.0 / D, None, ALU.mult))
                ch.link(nc.vector.tensor_tensor(WC[:, :, :], WR, rowm.unsqueeze(2).broadcast_to([D, L, D]),
                                                ALU.subtract))
                at = attb[:, :].rearrange("p (l f) -> p l f", l=L)
                for n, (w, o) in enumerate(((WR, SD[:, :, 0]), (WR, SD[:, :, 1]), (WER, VE[:, :]))):
                    dve.wait_ge(s_att, 16 * (n + 1))
                    nc.vector.tensor_tensor(PR, w, at, ALU.mult).then_inc(s_attf, 1)
                    dve.wait_ge(s_attf, n + 1)
                    ch.link(nc.vector.tensor_reduce(o, PR, AX.X, ALU.add))
                ch.link(nc.vector.tensor_reduce(bm[:, 0:L], brow[:, 0:L, :], AX.X, ALU.add))
                ch.link(nc.vector.tensor_scalar(bm[:, 0:L], bm[:, 0:L], 1.0 / D, None, ALU.mult))
                ch.link(nc.vector.tensor_tensor(brow[:, 0:L, :], brow[:, 0:L, :],
                                                bm[:, 0:L].unsqueeze(2).broadcast_to([1, L, D]), ALU.subtract))
                ch.link(nc.vector.tensor_copy(bpart[:, 0, :, :], brow))
                ch.link(nc.vector.tensor_tensor(blo, brow, bpart[:, 0, :, :], ALU.subtract))
                ch.link(nc.vector.tensor_copy(bpart[:, 1, :, :], blo))
                ch.link(nc.vector.tensor_tensor(blo, blo, bpart[:, 1, :, :], ALU.subtract))
                nc.vector.tensor_copy(bpart[:, 2, :, :], blo).then_inc(s_bs, 1)
                dve.wait_ge(s_meta, 64)
                dve.wait_ge(s_id, 1)
                ch.link(nc.vector.tensor_copy(DF, DH))
                cur = DF[:, 1:C + 1]
                ch.add(nc.vector.tensor_tensor(keep[:, :], cur, DF[:, 0:C], ALU.is_equal))
                ch.add(nc.vector.tensor_tensor(rep[:, :], cur, DF[:, 2:C + 2], ALU.not_equal))
                ch.add(nc.vector.tensor_tensor(knext[:, :], cur, DF[:, 2:C + 2], ALU.is_equal))
                ch.add(nc.vector.tensor_scalar(first[:, :], cur, DF[:, 1:2], None, ALU.is_equal))
                ch.add(nc.vector.tensor_scalar(last[:, :], cur, DF[:, C:C + 1], None, ALU.is_equal))
                ch.wait()
                ch.add(nc.vector.tensor_scalar(pen[:, :], keep[:, :], -1.0, BIG, ALU.add, ALU.mult))
                ch.add(nc.vector.tensor_scalar(penf[:, :], first[:, :], -1.0, BIG, ALU.add, ALU.mult))
                ch.link(nc.vector.tensor_scalar(tmp[:, :], cur, -float(NOWHERE), None, ALU.add))
                ch.link(nc.vector.tensor_tensor(tmp[:, :], tmp[:, :], rep[:, :], ALU.mult))
                ch.link(nc.vector.tensor_scalar(tmp[:, :], tmp[:, :], float(NOWHERE), None, ALU.add))
                ch.link(nc.vector.tensor_copy(repI[:, :], tmp[:, :]))
                nc.vector.tensor_scalar(DG[:, :], ident[0:P, 0:P], DF[:, 1:2], None, ALU.mult).then_inc(s_diag, 1)
                dve.wait_ge(s_bc, 1)
                ch.link(nc.vector.scalar_tensor_tensor(MF[:, :], PZ[0][0:P, 0, 0:P], DF[:, C:C + 1], MF[:, :],
                                                       ALU.is_equal, ALU.mult))
                nc.vector.tensor_scalar(DG[:, :], ident[0:P, 0:P], DF[:, C:C + 1], None, ALU.mult).then_inc(s_diag, 1)
                dve.wait_ge(s_bc, 2)
                ch.link(nc.vector.scalar_tensor_tensor(MB[:, :], PZ[1][0:P, 0, 0:P], DF[:, 1:2], MB[:, :],
                                                       ALU.is_equal, ALU.mult))
                ch.link(nc.vector.tensor_scalar(PM[:, :], MB[:, :], -1.0, BIG, ALU.add, ALU.mult))

        class Segments:

            def __init__(self, dve):
                self.dve, self.ch = dve, Chain(dve, "segment_chain")
                self.asked, self.carried = signal("carry_asked", "carried")
                self.n = 0

            def carry(self, ins):
                self.n += 1
                ins.then_inc(self.asked.s, 1)
                self.dve.wait_ge(*self.carried.at(self.n))

            def end(self):
                self.ch.end()
                self.asked.base += self.n
                self.carried.base += self.n

            def total(self, o, v):
                self.carry(nc.vector.tensor_tensor_scan(o, keep[:, :], v, 0.0, ALU.mult, ALU.add))
                self.ch.link(nc.vector.tensor_copy(car1[:, 0:1], PZ[3][0:P, 0, 0:1]))
                self.ch.link(nc.vector.scalar_tensor_tensor(o, first[:, :], car1[:, 0:1], o, ALU.mult, ALU.add))

            def spread(self, o, v, t):
                self.ch.link(nc.vector.tensor_tensor(t, v, rep[:, :], ALU.mult))
                self.carry(nc.vector.tensor_tensor_scan(o[:, ::-1], knext[:, ::-1], t[:, ::-1], 0.0,
                                                        ALU.mult, ALU.add))
                self.ch.link(nc.vector.tensor_copy(car1[:, 0:1], PZ[3][0:P, 0, 0:1]))
                self.ch.link(nc.vector.scalar_tensor_tensor(o, last[:, :], car1[:, 0:1], o, ALU.mult, ALU.add))

            def maximum(self, o, v):
                ch = self.ch
                ch.link(nc.vector.tensor_tensor_scan(o, pen[:, :], v, -BIG, ALU.add, ALU.max))
                self.carry(nc.vector.tensor_scalar(DG[:, :], ident[0:P, 0:P], o[:, C - 1:C], None, ALU.mult))
                ch.link(nc.vector.tensor_tensor(DG[:, :], PZ[3][0:P, 0, 0:P], PM[:, :], ALU.add))
                ch.link(nc.vector.tensor_reduce(car1[:, 0:1], DG[:, :], AX.X, ALU.max))
                ch.link(nc.vector.tensor_scalar(tmp[:, :], penf[:, :], car1[:, 0:1], None, ALU.add))
                ch.link(nc.vector.tensor_tensor(o, o, tmp[:, :], ALU.max))

        def carries(pe, seg, steps):
            for n, (kind, o) in enumerate(steps):
                pe.wait_ge(*seg.asked.at(n + 1))
                if kind == "total":
                    ins = nc.tensor.matmul(PZ[3][0:P, 0, 0:1], MF[:, :], o[:, C - 1:C], start=True, stop=True)
                elif kind == "spread":
                    ins = nc.tensor.matmul(PZ[3][0:P, 0, 0:1], MB[:, :], o[:, 0:1], start=True, stop=True)
                else:
                    ins = nc.tensor.matmul(PZ[3][0:P, 0, 0:P], ones[0:P, 0:P], DG[:, :], start=True, stop=True)
                ins.then_inc(seg.carried.s, 1)

        s_deg = sem("info_ready")
        s_degm = sem("degree_ready")
        s_degr = sem("degree_root_ready")
        s_eaT = sem("edge_attr_transposed")
        s_eac = sem("edge_attr_transposed_copied")
        s_aep = sem("edge_term_ready")
        s_aes = sem("edge_term_stored")
        EG = C // Q
        XSRC_EARLY = C // 2
        with nc.Block() as block:
            segbox = []

            @block.gpsimd
            def _(pool):
                gather_x(pool, S, srcI, 0, XSRC_EARLY, s_xsrc)

            @block.vector
            def _(dve):
                seg = Segments(dve)
                segbox.append(seg)
                ch = seg.ch
                ch.link(nc.vector.memset(lg[:, :], 1.0))
                seg.total(run[:, :], lg[:, :])
                nc.vector.tensor_scalar(lg[:, :], run[:, :], 1.0, None, ALU.max).then_inc(s_degm, 1)
                dve.wait_ge(s_degr, 1)
                ch.link(nc.vector.reciprocal(mx[:, :], ls[:, :]))
                nc.vector.tensor_copy(INFO[:, :, 1], mx[:, :]).then_inc(s_deg, 1)
                seg.spread(isq[:, :], mx[:, :], tmp[:, :])
                ch.link(nc.vector.reciprocal(mx[:, :], lg[:, :]))
                for g in range(EG):
                    dve.wait_ge(s_aep, g + 1)
                    nc.vector.tensor_copy(AE[:, g * Q:(g + 1) * Q, :],
                                          PZ[g % 2][0:P, 0, 0:Q * L].rearrange("p (a l) -> p a l", a=Q)).then_inc(s_aes, 1)
                dve.wait_ge(s_aes, EG)
                for l in range(L):
                    ch.link(nc.vector.tensor_copy(ls[:, :], AE[:, :, l]))
                    seg.total(lg[:, :], ls[:, :])
                    ch.link(nc.vector.tensor_tensor(AL[:, :, l], lg[:, :], mx[:, :], ALU.mult))

            @block.tensor
            def _(pe):
                seg = segbox[0]
                carries(pe, seg, [("total", run[:, :]), ("spread", isq[:, :])])
                pe.wait_ge(s_ea, 32)
                for g in range(EG):
                    if g >= 2:
                        pe.wait_ge(s_eac, g - 1)
                    transposes(PT[g % 2], [R[:, 1 + g * Q + a, :] for a in range(Q)]).then_inc(s_eaT, 1)
                    pe.wait_ge(s_eac, g + 1)
                    if g >= 2:
                        pe.wait_ge(s_aes, g - 1)
                    for a in range(Q):
                        ins = nc.tensor.matmul(PZ[g % 2][0:P, 0, a * L:(a + 1) * L],
                                               XT[:, g % 2, a * P:(a + 1) * P], VE[:, :], start=True, stop=True)
                    ins.then_inc(s_aep, 1)
                for l in range(L):
                    pe.wait_ge(*seg.asked.at(3 + l))
                    nc.tensor.matmul(PZ[3][0:P, 0, 0:1], MF[:, :], lg[:, C - 1:C], start=True,
                                     stop=True).then_inc(seg.carried.s, 1)

            @block.scalar
            def _(act):
                act.wait_ge(s_degm, 1)
                nc.scalar.activation(ls[:, :], lg[:, :], ACT.Sqrt).then_inc(s_degr, 1)
                for g in range(EG):
                    act.wait_ge(s_eaT, g + 1)
                    if g >= 2:
                        act.wait_ge(s_aep, g - 1)
                    nc.scalar.activation(XT[:, g % 2, :], PT[g % 2][:, 0:Q * P], ACT.Copy).then_inc(s_eac, 1)

        segbox[0].end()

        def dense(first_round, rounds, gathers):
            loaded = signal("x_loaded_0", "x_loaded_1")
            stored = signal("out_stored_0", "out_stored_1")
            y_ready, t_done, xt_ready, z_done, slope_ready, sq_ready, var_ready, rt_ready, out_ready = signal(
                "rows_ready", "transposed", "xt_ready", "product_done", "slope_ready", "squares_ready",
                "variance_ready", "root_ready", "out_ready")
            STEPS = 2 + L - 1
            K = STEPS * NS
            V = (2 + L) * NS

            chains = []

            with nc.Block() as block:
                @block.gpsimd
                def _(pool):
                    gathers(pool)

                @block.sync
                def _(sp):
                    for i in range(rounds + 2):
                        if i >= 2:
                            sp.wait_ge(*out_ready.at((i - 1) * NS))
                            dma2(sp, out_v[first_round + i - 2], X[:, i % 2, :, :], stored[i % 2].s)
                            sp.wait_ge(*stored[i % 2].at(32 * (i // 2)))
                        if i < rounds:
                            dma2(sp, X[:, i % 2, :, :], x_v[first_round + i], loaded[i % 2].s)

                @block.tensor
                def _(pe):
                    def turn(i, b):
                        for k in range(STEPS):
                            for s in range(NS):
                                pe.wait_ge(*y_ready.at(i * K + (k * NS + s + 1)))
                                transposes(PT[s], [Y[:, s, a, :] for a in range(Q)]).then_inc(t_done.s, 1)
                            for s in range(NS):
                                pe.wait_ge(*xt_ready.at(i * K + (k * NS + s + 1)))
                                w, bias = (W0[:, :], L) if k == 0 else (WC[:, k - 1, :], k - 1)
                                products(PZ[s], XT[:, s, :], w, bias).then_inc(z_done.s, 1)
                    pairs(pe, rounds, turn)

                @block.scalar
                def _(act):
                    def turn(i, b):
                        def root(k, s):
                            act.wait_ge(*var_ready.at(i * V + (k * NS + s + 1)))
                            v = mv[:, s, :, 1] if k < 2 else ss[:, s, :]
                            roots(v, s).then_inc(rt_ready.s, 1)

                        for s in range(NS):
                            root(0, s)
                        for k in range(STEPS):
                            for s in range(NS):
                                act.wait_ge(*t_done.at(i * K + (k * NS + s + 1)))
                                if k < 2:
                                    ins = nc.scalar.activation(XT[:, s, :], PT[s][:, 0:Q * P], ACT.Relu)
                                else:
                                    ins = nc.scalar.activation(XT[:, s, :], PT[s][:, 0:Q * P], ACT.Identity,
                                                               bias=BC[:, k - 2:k - 1], scale=GC[:, k - 2:k - 1])
                                ins.then_inc(xt_ready.s, 1)
                            for s in range(NS):
                                act.wait_ge(*z_done.at(i * K + (k * NS + s + 1)))
                                if k == 0:
                                    nc.scalar.mul(Y[:, s, :, :], PZ[s][0:P, :, :], 0.01).then_inc(slope_ready.s, 1)
                                else:
                                    nc.scalar.activation(Y[:, s, :, :], PZ[s][0:P, :, :], ACT.Square,
                                                         scale=D ** -0.5).then_inc(sq_ready.s, 1)
                                if s:
                                    root(k + 1, s - 1)
                            root(k + 1, NS - 1)
                    pairs(act, rounds, turn)

                @block.vector
                def _(dve):
                    per = NS * (2 * LN_LINKS + 2 + L + Q + 1)
                    chains.append(Chain(dve, "dense_chain", per))
                    ch = chains[0]

                    def turn(i, b):
                        ch.turn(i)
                        dve.wait_ge(*loaded[b].at((i - b) * 16 + 32))

                        def cols_of(s):
                            return X[:, b, s * Q:(s + 1) * Q, :]

                        def wait_root(k, s):
                            dve.wait_ge(*rt_ready.at(i * V + (k * NS + s + 1)))

                        for s in range(NS):
                            row_stats(ch, cols_of(s), s, var_ready.s)
                        for s in range(NS):
                            wait_root(0, s)
                            row_normal(ch, cols_of(s), Y[:, s, :, :], s, y_ready.s)
                        for s in range(NS):
                            dve.wait_ge(*slope_ready.at(i * NS + (s + 1)))
                            ch.link(nc.vector.tensor_tensor(Y[:, s, :, :], Y[:, s, :, :], PZ[s][0:P, :, :], ALU.max))
                            ch.link(nc.vector.tensor_tensor(cols_of(s), cols_of(s), Y[:, s, :, :], ALU.add))
                            row_stats(ch, cols_of(s), s, var_ready.s)
                        for s in range(NS):
                            wait_root(1, s)
                            row_normal(ch, cols_of(s), Y[:, s, :, :], s, y_ready.s)
                        for l in range(L):
                            for s in range(NS):
                                dve.wait_ge(*sq_ready.at(i * (L * NS) + (l * NS + s + 1)))
                                nc.vector.tensor_reduce(ss[:, s, :], Y[:, s, :, :], AX.X,
                                                        ALU.add).then_inc(var_ready.s, 1)
                            for s in range(NS):
                                wait_root(l + 2, s)
                                ch.link(nc.vector.reciprocal(rr[:, s, :], rt[:, s, :]))
                                if l < L - 1:
                                    nc.vector.tensor_tensor(Y[:, s, :, :], PZ[s][0:P, :, :],
                                                            wide(rr[:, s, :]), ALU.mult).then_inc(y_ready.s, 1)
                                    continue
                                for a in range(Q):
                                    ch.add(nc.vector.scalar_tensor_tensor(
                                        Y[:, s, a, :], PZ[s][0:P, a, :], rr[:, s, a:a + 1], G3[:, :],
                                        ALU.mult, ALU.mult))
                                ch.wait()
                                ch.link(nc.vector.tensor_tensor(
                                    Y[:, s, :, :], Y[:, s, :, :],
                                    B3[:, :].unsqueeze(1).broadcast_to([P, Q, D]), ALU.add))
                                nc.vector.tensor_tensor(cols_of(s), cols_of(s), Y[:, s, :, :],
                                                        ALU.add).then_inc(out_ready.s, 1)
                        assert ch.n == per
                    pairs(dve, rounds, turn)

            chains[0].end(chains[0].per * rounds)
            for sig, each in ((y_ready, K), (t_done, K), (xt_ready, K), (z_done, K), (slope_ready, NS),
                              (sq_ready, L * NS), (var_ready, V), (rt_ready, V), (out_ready, NS)):
                sig.base += each * rounds
            for b in range(2):
                loaded[b].base += 32 * ((rounds - b + 1) // 2)
                stored[b].base += 32 * ((rounds - b + 1) // 2)

        def turns(eng, full, ns_full, ns_last, turn, unrolled=False):
            if unrolled:
                for i in range(full):
                    turn(i, ns_full)
            else:
                with eng.Fori(0, full) as i:
                    turn(i, ns_full)
            turn(full, ns_last)

        def group(buf, i, per, s, shift=0):
            if isinstance(i, int):
                c = i * per + s * Q + shift
                return buf[:, c:c + Q]
            return buf[:, bass.ds(i * per + (s * Q + shift), Q)]

        def column(buf, i, per, c):
            if isinstance(i, int):
                return buf[:, i * per + c]
            v = buf[:, bass.ds(i * per + c, 1)]
            return v.rearrange("p a f -> p (a f)") if len(v.shape) == 3 else v

        def scalar_of(buf, i, per, c):
            return buf[:, i * per + c:i * per + c + 1] if isinstance(i, int) else buf[:, bass.ds(i * per + c, 1)]

        W4 = NS * Q
        FULL4, LAST4 = C // W4, C % W4 // Q

        def run_columns(ch, i, s):
            for a in range(Q):
                c = s * Q + a
                ch.link(nc.vector.scalar_tensor_tensor(
                    column(R, i, W4, c + 1), column(R, i, W4, c), scalar_of(keep, i, W4, c),
                    column(R, i, W4, c + 1), ALU.mult, ALU.add))

        def carry_in():
            brought = signal("carry_product")
            with nc.Block() as block:
                @block.tensor
                def _(pe):
                    nc.tensor.matmul(PZ[0][0:P, 0, :], MF[:, :], R[:, C, :], start=True, stop=True).then_inc(brought.s, 1)

                @block.scalar
                def _(act):
                    act.wait_ge(*brought.at(1))
                    nc.scalar.activation(CAR[:, :], PZ[0][0:P, 0, :], ACT.Copy)
            brought.base += 1

        s_iscat = sem("info_scattered")
        s_igat = sem("info_gathered")

        def first_gathers(pool):
            gather_x(pool, S, srcI, XSRC_EARLY, C, s_xsrc)
            for c in range(C):
                scatter(pool, info_t, repI[:, c:c + 1], N, INFO[:, c, :], s_iscat)
            gather_x(pool, T, dstI, 0, C, s_xdst)
            pool.wait_ge(s_iscat, 16 * C)
            for c in range(C):
                gather(pool, INFG[:, c, :], srcI[:, c:c + 1], info_t, N, s_igat)
            pool.wait_ge(s_xsrc, 16 * C)
            pool.wait_ge(s_xdst, 16 * C)
            pool.wait_ge(s_igat, 16 * C)

        dense(0, SHARES[0], first_gathers)

        s_alpha = sem("conv_alpha_ready")
        y_ready, t_done, xt_ready, z_done, m_ready, biased, slope_ready, s_ready, var_ready, rt_ready = (
            sem("convS_" + n) for n in ("rows_ready", "transposed", "xt_ready", "product_done",
                                        "message_ready", "bias_added", "slope_ready", "rows_final",
                                        "variance_ready", "root_ready"))
        with nc.Block() as block:
            @block.tensor
            def _(pe):
                def turn(i, ns):
                    for s in range(ns):
                        pe.wait_ge(y_ready, i * NS + (s + 1))
                        transposes(PT[s], [Y[:, s, a, :] for a in range(Q)]).then_inc(t_done, 1)
                    for s in range(ns):
                        pe.wait_ge(xt_ready, i * NS + (s + 1))
                        products(PZ[s], XT[:, s, :], W0[:, :], None).then_inc(z_done, 1)
                    for s in range(ns):
                        pe.wait_ge(m_ready, i * NS + (s + 1))
                        nc.tensor.matmul(PZ[s][0:P, :, :], ones3[:, 0:P], BR[:, L:L + 1, :].broadcast_to([3, Q, D]),
                                         start=False, stop=True, skip_group_check=True).then_inc(biased, 1)
                turns(pe, FULL4, NS, LAST4, turn)

            @block.scalar
            def _(act):
                act.wait_ge(s_alpha, 1)

                def turn(i, ns):
                    for s in range(ns):
                        act.wait_ge(var_ready, i * 2 * NS + (s + 1))
                        roots(mv[:, s, :, 1], s).then_inc(rt_ready, 1)
                    for s in range(ns):
                        act.wait_ge(t_done, i * NS + (s + 1))
                        nc.scalar.activation(XT[:, s, :], PT[s][:, 0:Q * P], ACT.Relu).then_inc(xt_ready, 1)
                    for s in range(ns):
                        act.wait_ge(z_done, i * NS + (s + 1))
                        for a in range(Q):
                            ins = nc.scalar.activation(column(R, i, W4, s * Q + a + 1), PZ[s][0:P, a, :], ACT.Copy,
                                                       scale=scalar_of(alpha, i, W4, s * Q + a))
                        ins.then_inc(m_ready, 1)
                    for s in range(ns):
                        act.wait_ge(biased, i * NS + (s + 1))
                        nc.scalar.mul(Y[:, s, :, :], PZ[s][0:P, :, :], 0.01).then_inc(slope_ready, 1)
                    for s in range(ns):
                        act.wait_ge(var_ready, i * 2 * NS + (ns + s + 1))
                        roots(mv[:, s, :, 1], s).then_inc(rt_ready, 1)
                turns(act, FULL4, NS, LAST4, turn)

            @block.vector
            def _(dve):
                c0 = Chain(dve, "convS_alpha_chain")
                c0.link(nc.vector.tensor_tensor(alpha[:, :], isq[:, :], wE[:, :], ALU.mult))
                nc.vector.tensor_tensor(alpha[:, :], alpha[:, :], INFG[:, :, 1], ALU.mult).then_inc(s_alpha, 1)
                ch = Chain(dve, "convS_chain", NS * (2 * LN_LINKS + 2 + Q))

                def turn(i, ns):
                    ch.turn(i)
                    for s in range(ns):
                        row_stats(ch, group(S, i, W4, s), s, var_ready)
                    for s in range(ns):
                        dve.wait_ge(rt_ready, i * 2 * NS + (s + 1))
                        row_normal(ch, group(S, i, W4, s), Y[:, s, :, :], s, y_ready)
                    for s in range(ns):
                        dve.wait_ge(m_ready, i * NS + (s + 1))
                        run_columns(ch, i, s)
                    for s in range(ns):
                        dve.wait_ge(slope_ready, i * NS + (s + 1))
                        sg = group(S, i, W4, s)
                        ch.link(nc.vector.tensor_tensor(Y[:, s, :, :], Y[:, s, :, :], PZ[s][0:P, :, :], ALU.max))
                        ch.link(nc.vector.tensor_tensor(sg, sg, Y[:, s, :, :], ALU.add))
                        row_stats(ch, sg, s, var_ready)
                    for s in range(ns):
                        dve.wait_ge(rt_ready, i * 2 * NS + (ns + s + 1))
                        sg = group(S, i, W4, s)
                        row_normal(ch, sg, sg, s, s_ready)
                turns(dve, FULL4, NS, LAST4, turn)

        carry_in()

        y_ready2, t_done2, xt_ready2, z_done2, x1_ready, t_ready, var_ready2, rt_ready2 = (
            sem("convT_" + n) for n in ("rows_ready", "transposed", "xt_ready", "product_done",
                                        "x1_ready", "rows_final",
                                        "variance_ready", "root_ready"))
        s_x1 = sem("x1_stored")
        s_rows = sem("rows_stored")

        with nc.Block() as block:
            @block.sync
            def _(sp):
                for i in range(FULL4 + 1):
                    c0, c1 = i * W4, min(C, (i + 1) * W4)
                    sp.wait_ge(x1_ready, c1 // Q)
                    dma2(sp, x1_v[:, c0:c1, :], R[:, c0 + 1:c1 + 1, :], s_x1)
                    sp.wait_ge(t_ready, c1 // Q)
                    dma2(sp, row_v[:, c0:c1, :], T[:, c0:c1, :], s_rows)
                sp.wait_ge(s_x1, 32 * (FULL4 + 1))
                sp.wait_ge(s_rows, 32 * (FULL4 + 1))

            @block.tensor
            def _(pe):
                def turn(i, ns):
                    for s in range(ns):
                        pe.wait_ge(y_ready2, i * NS + (s + 1))
                        transposes(PT[s], [Y[:, s, a, :] for a in range(Q)]).then_inc(t_done2, 1)
                    for s in range(ns):
                        pe.wait_ge(xt_ready2, i * NS + (s + 1))
                        products(PZ[s], XT[:, s, :], W0[:, :], L).then_inc(z_done2, 1)
                turns(pe, FULL4, NS, LAST4, turn)

            @block.scalar
            def _(act):
                def turn(i, ns):
                    for s in range(ns):
                        act.wait_ge(var_ready2, i * 2 * NS + (s + 1))
                        roots(mv[:, s, :, 1], s).then_inc(rt_ready2, 1)
                    for s in range(ns):
                        act.wait_ge(t_done2, i * NS + (s + 1))
                        nc.scalar.activation(XT[:, s, :], PT[s][:, 0:Q * P], ACT.Relu).then_inc(xt_ready2, 1)
                    for s in range(ns):
                        act.wait_ge(var_ready2, i * 2 * NS + (ns + s + 1))
                        roots(mv[:, s, :, 1], s).then_inc(rt_ready2, 1)
                turns(act, FULL4, NS, LAST4, turn)

            @block.vector
            def _(dve):
                ch = Chain(dve, "convT_chain", NS * (2 * LN_LINKS + Q + 2))

                def turn(i, ns):
                    ch.turn(i)
                    for s in range(ns):
                        row_stats(ch, group(T, i, W4, s), s, var_ready2)
                    for s in range(ns):
                        dve.wait_ge(rt_ready2, i * 2 * NS + (s + 1))
                        row_normal(ch, group(T, i, W4, s), Y[:, s, :, :], s, y_ready2)
                    for s in range(ns):
                        for a in range(Q):
                            c = s * Q + a
                            ch.add(nc.vector.scalar_tensor_tensor(
                                column(R, i, W4, c + 1), CAR[:, :], scalar_of(first, i, W4, c),
                                column(R, i, W4, c + 1), ALU.mult, ALU.add))
                        ch.wait()
                        dve.wait_ge(z_done2, i * NS + (s + 1))
                        rg = group(R, i, W4, s, 1)
                        tg = group(T, i, W4, s)
                        ch.link(nc.vector.tensor_tensor(rg, rg, PZ[s][0:P, :, :], ALU.add))
                        ch.link(leaky(Y[:, s, :, :], rg, 0.01))
                        nc.vector.tensor_tensor(rg, tg, Y[:, s, :, :], ALU.add).then_inc(x1_ready, 1)
                        dve.wait_ge(x1_ready, i * NS + (s + 1))
                        row_stats(ch, rg, s, var_ready2)
                    for s in range(ns):
                        dve.wait_ge(rt_ready2, i * 2 * NS + (ns + s + 1))
                        row_normal(ch, group(R, i, W4, s, 1), group(T, i, W4, s), s, t_ready)
                turns(dve, FULL4, NS, LAST4, turn)

        s_refresh = sem("s_refreshed")

        def refresh(n):
            def run(pool):
                for c in range(C):
                    gather(pool, S[:, c, :], INFG[:, c, 0:1].bitcast(I32), row_t, E, s_refresh)
                pool.wait_ge(s_refresh, 16 * C * n)
            return run

        W2 = 2 * Q
        FULL2 = C // W2
        s_x1b = sem("x1_loaded")
        s_out = sem("out_scattered")

        def attention(l):
            final = l == L - 1

            t_done, xt_ready, z_done, sq_ready, var_ready, rt_ready, copied, scaled = signal(
                "transposed", "xt_ready", "product_done", "squares_ready", "variance_ready", "root_ready",
                "message_copied", "rows_scaled")
            chains = []
            with nc.Block() as block:
                def streams(ns):
                    return range(NS) if ns == NS else (0, 2)

                def order(i, n):
                    return i * NS + (n + 1)

                @block.tensor
                def _(pe):
                    def turn(i, ns):
                        for n, s in enumerate(streams(ns)):
                            buf, g = (S, s) if s < 2 else (T, s - 2)
                            if i:
                                pe.wait_ge(*scaled.at(order(i - 1, s)))
                            c = i * W2 + g * Q
                            transposes(PT[s], [buf[:, c + a, :] for a in range(Q)]).then_inc(t_done.s, 1)
                        for n, s in enumerate(streams(ns)):
                            pe.wait_ge(*xt_ready.at(order(i, n)))
                            if s < 2 and i:
                                pe.wait_ge(*copied.at((i - 1) * 2 + s + 1))
                            for a in range(Q):
                                nc.tensor.matmul(PT[s][0:P, 500 + 2 * a:502 + 2 * a], XT[:, s, a * P:(a + 1) * P],
                                                 SD[:, l, :], start=True, stop=True, skip_group_check=True)
                            products(PZ[s], XT[:, s, :], WC[:, l, :], l).then_inc(z_done.s, 1)
                    turns(pe, FULL2, NS, 2, turn, unrolled=True)

                @block.scalar
                def _(act):
                    def turn(i, ns):
                        for n, s in enumerate(streams(ns)):
                            act.wait_ge(*t_done.at(order(i, n)))
                            if l == 0:
                                ins = nc.scalar.activation(XT[:, s, :], PT[s][:, 0:Q * P], ACT.Relu)
                            else:
                                ins = nc.scalar.activation(XT[:, s, :], PT[s][:, 0:Q * P], ACT.Identity,
                                                           bias=BC[:, l - 1:l], scale=GC[:, l - 1:l])
                            ins.then_inc(xt_ready.s, 1)
                        for n, s in enumerate(streams(ns)):
                            if s >= 2:
                                continue
                            act.wait_ge(*z_done.at(order(i, n)))
                            if not final:
                                nc.scalar.activation(Y[:, s, :, :], PZ[s][0:P, :, :], ACT.Square,
                                                     scale=D ** -0.5).then_inc(sq_ready.s, 1)
                            nc.scalar.activation(group(R, i, W2, s, 1), PZ[s][0:P, :, :],
                                                 ACT.Copy).then_inc(copied.s, 1)
                            if not final:
                                act.wait_ge(*var_ready.at(i * 2 + (n + 1)))
                                roots(ss[:, s, :], s).then_inc(rt_ready.s, 1)
                    turns(act, FULL2, NS, 2, turn)

                @block.vector
                def _(dve):
                    ch = Chain(dve, "project_chain", 2 if final else 6)
                    chains.append(ch)

                    def turn(i, ns):
                        ch.turn(i)
                        for n, s in enumerate(streams(ns)):
                            dve.wait_ge(*z_done.at(order(i, n)))
                            sc, g = (SCS, s) if s < 2 else (SCT, s - 2)
                            ins = nc.vector.tensor_copy(group(sc, i, W2, g), PT[s][0:P, 500:508]
                                                        .rearrange("p (a k) -> p a k", k=2))
                            if s >= 2:
                                ch.add(ins)
                                nc.vector.tensor_copy(group(T, i, W2, g), PZ[s][0:P, :, :]).then_inc(scaled.s, 1)
                            elif final:
                                ins.then_inc(scaled.s, 1)
                            else:
                                ch.add(ins)
                                dve.wait_ge(*sq_ready.at(i * 2 + (n + 1)))
                                nc.vector.tensor_reduce(ss[:, s, :], Y[:, s, :, :], AX.X,
                                                        ALU.add).then_inc(var_ready.s, 1)
                                dve.wait_ge(*rt_ready.at(i * 2 + (n + 1)))
                                ch.link(nc.vector.reciprocal(rr[:, s, :], rt[:, s, :]))
                                nc.vector.tensor_tensor(group(S, i, W2, g), PZ[s][0:P, :, :], wide(rr[:, s, :]),
                                                        ALU.mult).then_inc(scaled.s, 1)
                    turns(dve, FULL2, NS, 2, turn)

            chains[0].end()
            for sig in (t_done, xt_ready, z_done, scaled):
                sig.base += 2 * C // Q
            copied.base += C // Q
            for sig in (sq_ready, var_ready, rt_ready):
                sig.base += 0 if final else C // Q

            act_in, act_out = signal("exponents_ready", "exp_done")
            segbox = []
            with nc.Block() as block:
                @block.vector
                def _(dve):
                    seg = Segments(dve)
                    segbox.append(seg)
                    ch = seg.ch

                    def op(o, a, b, f):
                        ch.link(nc.vector.tensor_tensor(o[:, :], a, b, f))

                    seg.spread(run[:, :], SCT[:, :, 1], tmp[:, :])
                    op(lg, SCS[:, :, 0], run[:, :], ALU.add)
                    op(lg, lg[:, :], AE[:, :, l], ALU.add)
                    ch.link(nc.vector.scalar_tensor_tensor(lg[:, :], lg[:, :], 0.2, lg[:, :], ALU.mult, ALU.max))
                    op(ls, SCT[:, :, 0], SCT[:, :, 1], ALU.add)
                    op(ls, ls[:, :], AL[:, :, l], ALU.add)
                    ch.link(nc.vector.scalar_tensor_tensor(ls[:, :], ls[:, :], 0.2, ls[:, :], ALU.mult, ALU.max))
                    seg.maximum(mx[:, :], lg[:, :])
                    op(mx, mx[:, :], ls[:, :], ALU.max)
                    seg.spread(run[:, :], mx[:, :], tmp[:, :])
                    op(lg, lg[:, :], run[:, :], ALU.subtract)
                    op(ls, ls[:, :], run[:, :], ALU.subtract)
                    nc.vector.tensor_scalar(ls[:, :], ls[:, :], 0.0, None, ALU.min).then_inc(act_in.s, 1)
                    dve.wait_ge(*act_out.at(2))
                    seg.total(run[:, :], alpha[:, :])
                    op(run, run[:, :], aself[:, :], ALU.add)
                    ch.link(nc.vector.tensor_scalar(run[:, :], run[:, :], 1e-16, None, ALU.add))
                    seg.spread(mx[:, :], run[:, :], tmp[:, :])
                    ch.link(nc.vector.reciprocal(mx[:, :], mx[:, :]))
                    op(alpha, alpha[:, :], mx[:, :], ALU.mult)
                    op(aself, aself[:, :], mx[:, :], ALU.mult)

                @block.tensor
                def _(pe):
                    carries(pe, segbox[0], [("spread", run[:, :]), ("max", None), ("spread", run[:, :]),
                                            ("total", run[:, :]), ("spread", mx[:, :])])

                @block.scalar
                def _(act):
                    act.wait_ge(*act_in.at(1))
                    nc.scalar.activation(alpha[:, :], lg[:, :], ACT.Exp).then_inc(act_out.s, 1)
                    nc.scalar.activation(aself[:, :], ls[:, :], ACT.Exp).then_inc(act_out.s, 1)

                @block.sync
                def _(sp):
                    if final:
                        dma2(sp, S, x1_v, s_x1b)
                        sp.wait_ge(s_x1b, 32)

            segbox[0].end()
            act_in.base += 1
            act_out.base += 2
            weighted = signal("messages_weighted")
            with nc.Block() as block:
                @block.scalar
                def _(act):
                    def turn(i, ns):
                        for s in range(ns):
                            for a in range(Q):
                                c = s * Q + a
                                ins = nc.scalar.activation(column(R, i, W4, c + 1), column(R, i, W4, c + 1), ACT.Copy,
                                                           scale=scalar_of(alpha, i, W4, c))
                            ins.then_inc(weighted.s, 1)
                    turns(act, FULL4, NS, LAST4, turn)

                @block.vector
                def _(dve):
                    ch = Chain(dve, "run_chain", NS * Q)
                    chains.append(ch)

                    def turn(i, ns):
                        ch.turn(i)
                        for s in range(ns):
                            dve.wait_ge(*weighted.at(i * NS + (s + 1)))
                            run_columns(ch, i, s)
                    turns(dve, FULL4, NS, LAST4, turn)

            carry_in()

            chains[1].end()
            weighted.base += C // Q

            sum_ready, sq_ready2, var_ready2, rt_ready2, t_ready = signal(
                "sum_ready", "squares_ready", "variance_ready", "root_ready", "t_rows_final")
            with nc.Block() as block:
                @block.vector
                def _(dve):
                    ch = Chain(dve, "t_chain", NS * (Q + 1 + (Q + 1 if final else 0)))
                    chains.append(ch)

                    def turn(i, ns):
                        ch.turn(i)
                        for s in range(ns):
                            for a in range(Q):
                                c = s * Q + a
                                ch.add(nc.vector.scalar_tensor_tensor(
                                    column(T, i, W4, c), column(T, i, W4, c), scalar_of(aself, i, W4, c),
                                    column(R, i, W4, c + 1), ALU.mult, ALU.add))
                            ch.wait()
                            for a in range(Q):
                                c = s * Q + a
                                ins = nc.vector.scalar_tensor_tensor(
                                    column(T, i, W4, c), CAR[:, :], scalar_of(first, i, W4, c),
                                    column(T, i, W4, c), ALU.mult, ALU.add)
                            ins.then_inc(sum_ready.s, 1)
                        for s in range(ns):
                            dve.wait_ge(*sq_ready2.at(i * NS + (s + 1)))
                            nc.vector.tensor_reduce(ss[:, s, :], Y[:, s, :, :], AX.X,
                                                    ALU.add).then_inc(var_ready2.s, 1)
                        for s in range(ns):
                            dve.wait_ge(*rt_ready2.at(i * NS + (s + 1)))
                            tg = group(T, i, W4, s)
                            ch.link(nc.vector.reciprocal(rr[:, s, :], rt[:, s, :]))
                            if not final:
                                nc.vector.tensor_tensor(tg, tg, wide(rr[:, s, :]), ALU.mult).then_inc(t_ready.s, 1)
                                continue
                            for a in range(Q):
                                c = s * Q + a
                                ch.add(nc.vector.scalar_tensor_tensor(
                                    column(T, i, W4, c), column(T, i, W4, c), rr[:, s, a:a + 1], G3[:, :],
                                    ALU.mult, ALU.mult))
                            ch.wait()
                            ch.link(nc.vector.tensor_tensor(tg, tg, B3[:, :].unsqueeze(1).broadcast_to([P, Q, D]),
                                                            ALU.add))
                            nc.vector.tensor_tensor(tg, tg, group(S, i, W4, s), ALU.add).then_inc(t_ready.s, 1)
                    turns(dve, FULL4, NS, LAST4, turn)

                @block.scalar
                def _(act):
                    def turn(i, ns):
                        for s in range(ns):
                            act.wait_ge(*sum_ready.at(i * NS + (s + 1)))
                            nc.scalar.activation(Y[:, s, :, :], group(T, i, W4, s), ACT.Square,
                                                 scale=D ** -0.5).then_inc(sq_ready2.s, 1)
                        for s in range(ns):
                            act.wait_ge(*var_ready2.at(i * NS + (s + 1)))
                            roots(ss[:, s, :], s).then_inc(rt_ready2.s, 1)
                    turns(act, FULL4, NS, LAST4, turn)

                if final:
                    @block.gpsimd
                    def _(pool):
                        for c in range(C):
                            pool.wait_ge(*t_ready.at(c // Q + 1))
                            scatter(pool, out, repI[:, c:c + 1], N, T[:, c, :], s_out)
                        pool.wait_ge(s_out, 16 * C)
                else:
                    @block.sync
                    def _(sp):
                        before = 32 * (FULL4 + 1) * (l + 1)
                        for i in range(FULL4 + 1):
                            c0, c1 = i * W4, min(C, (i + 1) * W4)
                            sp.wait_ge(*t_ready.at(c1 // Q))
                            dma2(sp, row_v[:, c0:c1, :], T[:, c0:c1, :], s_rows)
                        sp.wait_ge(s_rows, before + 32 * (FULL4 + 1))

            chains[2].end()
            for sig in (sum_ready, sq_ready2, var_ready2, rt_ready2, t_ready):
                sig.base += C // Q

        done = SHARES[0]
        for l in range(L):
            dense(done, SHARES[l + 1], refresh(l + 1))
            done += SHARES[l + 1]
            attention(l)
        assert done == ROUNDS


_INS = ["x", "src", "dst", "edge_attr_128", "edge_weight", "L0_gnn_W_weight", "L0_gnn_W_bias", "L1_gnn_W",
        "L1_gnn_We", "L1_gnn_att_src", "L1_gnn_att_dst", "L1_gnn_att_edge", "L1_gnn_bias",
        "L1_gnn_ln_gamma", "L1_gnn_ln_beta"]


def kernel(**inputs):
    import numpy as np
    import concourse.bacc as bacc
    from concourse.bass_utils import run_bass_kernel_spmd

    nc = bacc.Bacc("TRN2", target_bir_lowering=False, num_devices=1)
    arrays, args = {}, []
    for name in _INS:
        a = np.ascontiguousarray(inputs[name])
        arrays["in_" + name] = a
        args.append(nc.dram_tensor("in_" + name, a.shape, mybir.dt.from_np(a.dtype), kind="ExternalInput").ap())
    out = nc.dram_tensor("out_rows", (N, D), F32, kind="ExternalOutput").ap()
    gnn_kernel(nc, *args, out)
    r = run_bass_kernel_spmd(nc, [arrays], core_ids=[0])
    return r.results[0]["out_rows"]
```

```python
import concourse.bass as bass
from concourse import mybir
from contextlib import ExitStack

F32 = mybir.dt.float32
I32 = mybir.dt.int32
BF16 = mybir.dt.bfloat16
ALU = mybir.AluOpType
ACT = mybir.ActivationFunctionType
AX = mybir.AxisListType

D = 128
N = 50000
E = 12500
L = 4
P = 125
C = E // P
Q = 4
NS = 4
DS = 5
ROUND = P * DS * Q
ROUNDS = N // ROUND
CORE = 112
EPS = 1e-5
BIG = 1e30
NOWHERE = 1 << 23
SHARES = [8, 3, 3, 3, 3]


def gnn_kernel(nc, x, src, dst, ea, ew, w0, b0, wg, we, att_s, att_d, att_e, bg, gamma, beta, out):
    ctx = ExitStack()
    with ctx:
        ctx.enter_context(nc.allow_non_contiguous_dma(reason="a few hundred single elements, once"))

        def sb(name, shape, dt=F32):
            return ctx.enter_context(nc.sbuf_tensor(name, shape, dt))

        def sem(name):
            return ctx.enter_context(nc.semaphore(name))

        class Signal:

            def __init__(self, name):
                self.s, self.base = sem(name), 0

            def at(self, n):
                return self.s, self.base + n

        signals = {}

        def signal(*names):
            for n in names:
                if n not in signals:
                    signals[n] = Signal(n)
            got = [signals[n] for n in names]
            return got if len(got) > 1 else got[0]

        S = sb("S", [P, C, D])
        T = sb("T", [P, C, D])
        R = sb("R", [P, C + 1, D])
        X = R[:, 1:1 + 2 * DS * Q, :].rearrange("p (b r) f -> p b r f", b=2)
        YB = sb("Y", [D, DS, Q, D])
        Y = YB[0:P, :, :, :]
        XT = sb("XT", [D, NS, Q * P])
        ident = sb("ident", [D, D])
        ones = sb("ones", [D, D])
        ones3 = sb("ones3", [3, D], BF16)
        W0 = sb("W0", [D, D])
        WC = sb("WC", [D, L, D])
        SD = sb("SD", [D, L, 2])
        VE = sb("VE", [D, L])
        BR = sb("BR", [3, L + 1, D], BF16)
        GC = sb("GC", [D, L])
        BC = sb("BC", [D, L])
        G3 = sb("G3", [P, D])
        B3 = sb("B3", [P, D])
        B0 = sb("B0", [P, D])
        MF = sb("MF", [P, P])
        MB = sb("MB", [P, P])
        PM = sb("PM", [P, P])
        DG = sb("DG", [P, P])
        CAR = sb("CAR", [P, D])

        def cols(name, dt=F32):
            return sb(name, [P, C], dt)

        keep, knext, rep, first, last, pen, penf = (cols(n) for n in (
            "keep", "knext", "rep", "first", "last", "pen", "penf"))
        srcI, dstI, repI = (cols(n, I32) for n in ("srcI", "dstI", "repI"))
        wE, lg, ls, run, mx, tmp, alpha, aself, isq = (cols(n) for n in (
            "wE", "lg", "ls", "run", "mx", "tmp", "alpha", "aself", "isq"))
        AE = sb("AE", [P, C, L])
        AL = sb("AL", [P, C, L])
        INFO = sb("INFO", [P, C, 2])
        INFG = sb("INFG", [P, C, 2])
        SCS = sb("SCS", [P, C, 2])
        SCT = sb("SCT", [P, C, 2])
        st = sb("st", [P, 2, Q, 6])
        mv = sb("mv", [P, DS, Q, 2])
        rt = sb("rt", [P, DS, Q])
        nm = sb("nm", [P, DS, Q])
        epsc = sb("epsc", [P, 1])
        taken = sb("taken", [P, 2])
        rr = sb("rr", [P, DS, Q])
        ss = sb("ss", [P, DS, Q])
        car1 = sb("car1", [P, L])

        banks = [ctx.enter_context(nc.psum_tensor(f"bank{b}", [D, 512], F32)) for b in range(8)]

        def tiles_of(bank):
            return bank[:, :].rearrange("p (a f) -> p a f", a=Q)

        PT, PZ = banks[0:4], [tiles_of(b) for b in banks[4:8]]
        DPT, DPZ = banks[0:3], [tiles_of(b) for b in banks[3:8]]

        info_t = nc.dram_tensor("info_t", [N, 2], F32, kind="Internal").ap()
        row_t = nc.dram_tensor("row_t", [E, D], F32, kind="Internal").ap()
        x1_t = nc.dram_tensor("x1_t", [E, D], F32, kind="Internal").ap()
        row_v = row_t.rearrange("(p c) f -> p c f", p=P)
        x1_v = x1_t.rearrange("(p c) f -> p c f", p=P)
        x_v = x.rearrange("(i p r) f -> i p r f", p=P, r=DS * Q)
        out_v = out.rearrange("(i p r) f -> i p r f", p=P, r=DS * Q)

        def dma2(eng, dst_ap, src_ap, s):
            eng.dma_start(dst_ap[0:CORE], src_ap[0:CORE]).then_inc(s, 16)
            eng.dma_start(dst_ap[CORE:P], src_ap[CORE:P]).then_inc(s, 16)

        class Chain:

            def __init__(self, dve, name, per=0):
                self.dve, self.done, self.per, self.n, self.base = dve, signal(name), per, 0, 0

            def turn(self, i):
                self.base, self.n = i * self.per, 0

            def add(self, ins):
                ins.then_inc(self.done.s, 1)
                self.n += 1

            def wait(self):
                self.dve.wait_ge(*self.done.at(self.base + self.n))

            def link(self, ins):
                self.add(ins)
                self.wait()

            def end(self, total=None):
                self.done.base += self.base + self.n if total is None else total

        def take_wait(n):
            nc.vector.memset(taken[:, n:n + 1], 0.0)

        def row_stats(ch, src4, s, ready):
            take_wait(0)
            for a in range(Q):
                ch.add(nc.vector.bn_stats(st[:, s % 2, a, :], src4[:, a, :]))
            ch.wait()
            take_wait(1)
            for a in range(Q):
                ins = nc.vector.bn_aggr(mv[:, s, a, :], st[:, s % 2, a, :])
            ins.then_inc(ready, 1)

        ACT_TILES = (2, 3)

        def row_scales(ch, s, ready):
            ch.link(nc.vector.reciprocal(rr[:, s, :], rt[:, s, :]))
            nc.vector.scalar_tensor_tensor(nm[:, s, :], mv[:, s, :, 0], -1.0, rr[:, s, :], ALU.mult,
                                           ALU.mult).then_inc(ready, 1)

        def row_normal(ch, src4, dst4, s, ready):
            ch.link(nc.vector.reciprocal(rr[:, s, :], rt[:, s, :]))
            for a in range(Q):
                ins = nc.vector.tensor_scalar(dst4[:, a, :], src4[:, a, :], mv[:, s, a, 0:1],
                                              rr[:, s, a:a + 1], ALU.subtract, ALU.mult)
            ins.then_inc(ready, 1)

        LN_LINKS = Q + 1

        def leaky(o, v, slope):
            return nc.vector.scalar_tensor_tensor(o, v, slope, v, ALU.mult, ALU.max)

        def roots(v, s):
            return nc.scalar.activation(rt[:, s, :], v, ACT.Sqrt, bias=epsc[:, 0:1])

        def wide(v, n=Q):
            return v.unsqueeze(2).broadcast_to([P, n, D])

        def transposes(ps, tiles):
            for a, t in enumerate(tiles):
                ins = nc.tensor.transpose(ps[:, a * P:(a + 1) * P], t, ident[0:P, 0:P])
            return ins

        def products(pz, xt, w, bias):
            if bias is not None:
                nc.tensor.matmul(pz[0:P, :, :], ones3[:, 0:P],
                                 BR[:, bias:bias + 1, :].broadcast_to([3, Q, D]),
                                 start=True, stop=False, skip_group_check=True)
            for a in range(Q):
                ins = nc.tensor.matmul(pz[0:P, a, :], xt[:, a * P:(a + 1) * P], w,
                                       start=bias is None and a == 0, stop=True, skip_group_check=True)
            return ins

        def gather(pool, to, idx, table, rows, done):
            pool.indirect_dma_start(to, None, table, bass.IndirectOffsetOnAxis(ap=idx, axis=0),
                                    bounds_check=rows - 1, oob_is_err=False).then_inc(done, 16)

        def scatter(pool, table, idx, rows, frm, done):
            pool.indirect_dma_start(table, bass.IndirectOffsetOnAxis(ap=idx, axis=0), frm, None,
                                    bounds_check=rows - 1, oob_is_err=False).then_inc(done, 16)

        def gather_x(pool, to, idx, c0, c1, done):
            for c in range(c0, c1):
                gather(pool, to[:, c, :], idx[:, c:c + 1], x, N, done)

        def pairs(eng, n, turn):
            if n >= 4:
                with eng.Fori(0, n // 2) as ii:
                    turn(ii * 2, 0)
                    turn(ii * 2 + 1, 1)
                rest = n // 2 * 2
            else:
                rest = 0
            for i in range(rest, n):
                turn(i, i % 2)

        s_w = sem("weights_loaded")
        s_meta = sem("edges_loaded")
        s_halo = sem("halo_cleared")
        s_id = sem("identity_ready")
        s_bs = sem("bias_split")
        s_br = sem("bias_rows_placed")
        s_wT = sem("w0_transposed")
        s_diag = sem("diagonal_ready")
        s_bc = sem("row_broadcast")
        s_ea = sem("edge_attr_loaded")
        s_fill = sem("info_filled")
        s_filled = sem("info_table_filled")
        s_idx = sem("indices_loaded")
        s_xsrc = sem("x_src_gathered")
        s_xdst = sem("x_dst_gathered")

        wide0 = XT[:, :, :].rearrange("p s q -> p (s q)")
        WR = wide0[:, 0:L * D].rearrange("p (l f) -> p l f", l=L)
        WER = wide0[:, 512:512 + L * D].rearrange("p (l f) -> p l f", l=L)
        PR = wide0[:, 1024:1024 + L * D].rearrange("p (l f) -> p l f", l=L)
        W0R = wide0[:, 1536:1536 + D]
        rowm = wide0[:, 1664:1664 + L]
        Yb = YB[:, :, :, :].rearrange("p s q f -> p (s q f)")
        attb = Yb[:, 1408:1408 + L * D]
        Yf = Yb[0:P]
        DH = Yf[:, 0:C + 2].bitcast(I32)
        DF = Yf[:, 128:128 + C + 2]
        brow = Yf[0:1, 256:256 + (L + 1) * D].rearrange("p (l f) -> p l f", l=L + 1)
        blo = X[0:1, 1, 8:8 + L + 1, :]
        bm = Yf[0:1, 1000:1000 + L + 1]
        bpart = X[0:1, 1, 0:8, :].rearrange("p a f -> p (a f)")[:, 0:960].bitcast(BF16) \
            .rearrange("p (k l f) -> p k l f", k=3, l=L + 1)
        fill = X[:, 0, :, :].rearrange("p a f -> p (a f)")[:, 0:800].rearrange("p (n k) -> p n k", k=2)

        with nc.Block() as block:
            @block.sync
            def _(sp):
                for a, b in ((WR, wg.rearrange("l k j -> k l j")), (WER, we.rearrange("l k j -> k l j")),
                             (W0R, w0), (GC[:, :], gamma.rearrange("l f -> f l")),
                             (BC[:, :], beta.rearrange("l f -> f l")),
                             (brow[:, 0:L, :], bg.unsqueeze(0)), (brow[:, L, :], b0.unsqueeze(0)),
                             (G3[:, :], gamma[L - 1:L, :].broadcast_to([P, D])),
                             (B3[:, :], beta[L - 1:L, :].broadcast_to([P, D])),
                             (B0[:, :], b0.unsqueeze(0).broadcast_to([P, D]))):
                    sp.dma_start(a, b).then_inc(s_w, 16)
                dv = dst.rearrange("(p c) -> p c", p=P)
                sp.wait_ge(s_halo, 1)
                sp.dma_start(DH[:, 1:C + 1], dv).then_inc(s_meta, 16)
                sp.dma_start(DH[1:P, 0:1], dv[0:P - 1, C - 1:C]).then_inc(s_meta, 16)
                sp.dma_start(DH[0:P - 1, C + 1:C + 2], dv[1:P, 0:1]).then_inc(s_meta, 16)
                sp.dma_start(wE[:, :], ew.rearrange("(p c) -> p c", p=P)).then_inc(s_meta, 16)
                sp.wait_ge(s_bs, 1)
                for k in range(3):
                    sp.dma_start(BR[k:k + 1, :, :], bpart[:, k, :, :]).then_inc(s_br, 16)
                sp.wait_ge(s_br, 48)
                sp.wait_ge(s_fill, 1)
                dma2(sp, info_t.rearrange("(p n) k -> p n k", p=P), fill, s_filled)
                sp.wait_ge(s_filled, 32)
                dma2(sp, R[:, 1:C + 1, :], ea.rearrange("(p c) f -> p c f", p=P), s_ea)
                sp.dma_start(srcI[:, :], src.rearrange("(p c) -> p c", p=P)).then_inc(s_idx, 16)
                sp.dma_start(dstI[:, :], dv).then_inc(s_idx, 16)
                sp.wait_ge(s_filled, 32)
                sp.wait_ge(s_idx, 32)

            s_att = sem("att_loaded")
            s_attf = sem("att_used")

            @block.scalar
            def _(act):
                for n, att in enumerate((att_s, att_d, att_e)):
                    if n:
                        act.wait_ge(s_attf, n)
                    act.dma_start(attb[:, :], att.rearrange("l f -> (l f)").unsqueeze(0)
                                  .broadcast_to([D, L * D])).then_inc(s_att, 16)
                act.wait_ge(s_att, 48)

            @block.gpsimd
            def _(pool):
                z1 = sem("zeros_set")
                nc.gpsimd.memset(ident[:, :], 0.0).then_inc(z1, 1)
                nc.gpsimd.memset(ones[:, :], 1.0)
                nc.gpsimd.memset(ones3[:, :], 1.0)
                nc.gpsimd.memset(epsc[:, :], EPS)
                nc.gpsimd.memset(MF[:, :], 1.0).then_inc(z1, 1)
                nc.gpsimd.memset(MB[:, :], 1.0).then_inc(z1, 1)
                pool.wait_ge(z1, 3)
                nc.gpsimd.affine_select(out=ident[:, :], in_=ident[:, :], compare_op=ALU.not_equal,
                                        fill=1.0, base=0, pattern=[[-1, D]], channel_multiplier=1)
                nc.gpsimd.affine_select(out=MF[:, :], in_=MF[:, :], compare_op=ALU.is_gt, fill=0.0,
                                        base=0, pattern=[[1, P]], channel_multiplier=-1)
                nc.gpsimd.affine_select(out=MB[:, :], in_=MB[:, :], compare_op=ALU.is_gt, fill=0.0,
                                        base=0, pattern=[[-1, P]], channel_multiplier=1)
                nc.gpsimd.iota(INFO[:, :, 0].bitcast(I32), pattern=[[1, C]], base=0,
                               channel_multiplier=C).then_inc(s_id, 1)

            @block.tensor
            def _(pe):
                pe.wait_ge(s_id, 1)
                pe.wait_ge(s_w, 160)
                nc.tensor.transpose(PT[0][:, 0:D], W0R, ident[:, :]).then_inc(s_wT, 1)
                for n in range(2):
                    pe.wait_ge(s_diag, n + 1)
                    nc.tensor.matmul(PZ[n][0:P, 0, 0:P], ones[0:P, 0:P], DG[:, :],
                                     start=True, stop=True).then_inc(s_bc, 1)

            @block.vector
            def _(dve):
                ch = Chain(dve, "setup_chain")
                ch.add(nc.vector.memset(R[:, 0, :], 0.0))
                ch.add(nc.vector.memset(DH[:, :], NOWHERE))
                ch.wait()
                nc.vector.memset(fill[:, :, 0].bitcast(I32), NOWHERE).then_inc(s_halo, 1)
                nc.vector.memset(fill[:, :, 1], 1.0).then_inc(s_fill, 1)
                dve.wait_ge(s_w, 160)
                dve.wait_ge(s_wT, 1)
                ch.link(nc.vector.tensor_copy(W0[:, :], PT[0][:, 0:D]))
                ch.link(nc.vector.tensor_reduce(rowm, WR, AX.X, ALU.add))
                ch.link(nc.vector.tensor_scalar(rowm, rowm, 1.0 / D, None, ALU.mult))
                ch.link(nc.vector.tensor_tensor(WC[:, :, :], WR, rowm.unsqueeze(2).broadcast_to([D, L, D]),
                                                ALU.subtract))
                at = attb[:, :].rearrange("p (l f) -> p l f", l=L)
                for n, (w, o) in enumerate(((WR, SD[:, :, 0]), (WR, SD[:, :, 1]), (WER, VE[:, :]))):
                    dve.wait_ge(s_att, 16 * (n + 1))
                    nc.vector.tensor_tensor(PR, w, at, ALU.mult).then_inc(s_attf, 1)
                    dve.wait_ge(s_attf, n + 1)
                    ch.link(nc.vector.tensor_reduce(o, PR, AX.X, ALU.add))
                ch.link(nc.vector.tensor_reduce(bm[:, 0:L], brow[:, 0:L, :], AX.X, ALU.add))
                ch.link(nc.vector.tensor_scalar(bm[:, 0:L], bm[:, 0:L], 1.0 / D, None, ALU.mult))
                ch.link(nc.vector.tensor_tensor(brow[:, 0:L, :], brow[:, 0:L, :],
                                                bm[:, 0:L].unsqueeze(2).broadcast_to([1, L, D]), ALU.subtract))
                ch.link(nc.vector.tensor_copy(bpart[:, 0, :, :], brow))
                ch.link(nc.vector.tensor_tensor(blo, brow, bpart[:, 0, :, :], ALU.subtract))
                ch.link(nc.vector.tensor_copy(bpart[:, 1, :, :], blo))
                ch.link(nc.vector.tensor_tensor(blo, blo, bpart[:, 1, :, :], ALU.subtract))
                nc.vector.tensor_copy(bpart[:, 2, :, :], blo).then_inc(s_bs, 1)
                dve.wait_ge(s_meta, 64)
                dve.wait_ge(s_id, 1)
                ch.link(nc.vector.tensor_copy(DF, DH))
                cur = DF[:, 1:C + 1]
                ch.add(nc.vector.tensor_tensor(keep[:, :], cur, DF[:, 0:C], ALU.is_equal))
                ch.add(nc.vector.tensor_tensor(rep[:, :], cur, DF[:, 2:C + 2], ALU.not_equal))
                ch.add(nc.vector.tensor_tensor(knext[:, :], cur, DF[:, 2:C + 2], ALU.is_equal))
                ch.add(nc.vector.tensor_scalar(first[:, :], cur, DF[:, 1:2], None, ALU.is_equal))
                ch.add(nc.vector.tensor_scalar(last[:, :], cur, DF[:, C:C + 1], None, ALU.is_equal))
                ch.wait()
                ch.add(nc.vector.tensor_scalar(pen[:, :], keep[:, :], -1.0, BIG, ALU.add, ALU.mult))
                ch.add(nc.vector.tensor_scalar(penf[:, :], first[:, :], -1.0, BIG, ALU.add, ALU.mult))
                ch.link(nc.vector.tensor_scalar(tmp[:, :], cur, -float(NOWHERE), None, ALU.add))
                ch.link(nc.vector.tensor_tensor(tmp[:, :], tmp[:, :], rep[:, :], ALU.mult))
                ch.link(nc.vector.tensor_scalar(tmp[:, :], tmp[:, :], float(NOWHERE), None, ALU.add))
                ch.link(nc.vector.tensor_copy(repI[:, :], tmp[:, :]))
                nc.vector.tensor_scalar(DG[:, :], ident[0:P, 0:P], DF[:, 1:2], None, ALU.mult).then_inc(s_diag, 1)
                dve.wait_ge(s_bc, 1)
                ch.link(nc.vector.scalar_tensor_tensor(MF[:, :], PZ[0][0:P, 0, 0:P], DF[:, C:C + 1], MF[:, :],
                                                       ALU.is_equal, ALU.mult))
                nc.vector.tensor_scalar(DG[:, :], ident[0:P, 0:P], DF[:, C:C + 1], None, ALU.mult).then_inc(s_diag, 1)
                dve.wait_ge(s_bc, 2)
                ch.link(nc.vector.scalar_tensor_tensor(MB[:, :], PZ[1][0:P, 0, 0:P], DF[:, 1:2], MB[:, :],
                                                       ALU.is_equal, ALU.mult))
                ch.link(nc.vector.tensor_scalar(PM[:, :], MB[:, :], -1.0, BIG, ALU.add, ALU.mult))

        class Segments:

            def __init__(self, dve):
                self.dve, self.ch = dve, Chain(dve, "segment_chain")
                self.asked, self.carried = signal("carry_asked", "carried")
                self.n = 0

            def carry(self, ins):
                self.n += 1
                ins.then_inc(self.asked.s, 1)
                self.dve.wait_ge(*self.carried.at(self.n))

            def end(self):
                self.ch.end()
                self.asked.base += self.n
                self.carried.base += self.n

            def total(self, o, v):
                self.carry(nc.vector.tensor_tensor_scan(o, keep[:, :], v, 0.0, ALU.mult, ALU.add))
                self.ch.link(nc.vector.tensor_copy(car1[:, 0:1], PZ[3][0:P, 0, 0:1]))
                self.ch.link(nc.vector.scalar_tensor_tensor(o, first[:, :], car1[:, 0:1], o, ALU.mult, ALU.add))

            def spread(self, o, v, t):
                self.ch.link(nc.vector.tensor_tensor(t, v, rep[:, :], ALU.mult))
                self.carry(nc.vector.tensor_tensor_scan(o[:, ::-1], knext[:, ::-1], t[:, ::-1], 0.0,
                                                        ALU.mult, ALU.add))
                self.ch.link(nc.vector.tensor_copy(car1[:, 0:1], PZ[3][0:P, 0, 0:1]))
                self.ch.link(nc.vector.scalar_tensor_tensor(o, last[:, :], car1[:, 0:1], o, ALU.mult, ALU.add))

            def maximum(self, o, v):
                ch = self.ch
                ch.link(nc.vector.tensor_tensor_scan(o, pen[:, :], v, -BIG, ALU.add, ALU.max))
                self.carry(nc.vector.tensor_scalar(DG[:, :], ident[0:P, 0:P], o[:, C - 1:C], None, ALU.mult))
                ch.link(nc.vector.tensor_tensor(DG[:, :], PZ[3][0:P, 0, 0:P], PM[:, :], ALU.add))
                ch.link(nc.vector.tensor_reduce(car1[:, 0:1], DG[:, :], AX.X, ALU.max))
                ch.link(nc.vector.tensor_scalar(tmp[:, :], penf[:, :], car1[:, 0:1], None, ALU.add))
                ch.link(nc.vector.tensor_tensor(o, o, tmp[:, :], ALU.max))

        def carries(pe, seg, steps):
            for n, (kind, o) in enumerate(steps):
                pe.wait_ge(*seg.asked.at(n + 1))
                if kind == "total":
                    ins = nc.tensor.matmul(PZ[3][0:P, 0, 0:1], MF[:, :], o[:, C - 1:C], start=True, stop=True)
                elif kind == "spread":
                    ins = nc.tensor.matmul(PZ[3][0:P, 0, 0:1], MB[:, :], o[:, 0:1], start=True, stop=True)
                else:
                    ins = nc.tensor.matmul(PZ[3][0:P, 0, 0:P], ones[0:P, 0:P], DG[:, :], start=True, stop=True)
                ins.then_inc(seg.carried.s, 1)

        s_deg = sem("info_ready")
        s_degm = sem("degree_ready")
        s_degr = sem("degree_root_ready")
        s_eaT = sem("edge_attr_transposed")
        s_eac = sem("edge_attr_transposed_copied")
        s_aep = sem("edge_term_ready")
        s_aes = sem("edge_term_stored")
        EG = C // Q
        XSRC_EARLY = C // 2
        with nc.Block() as block:
            segbox = []

            @block.gpsimd
            def _(pool):
                gather_x(pool, S, srcI, 0, XSRC_EARLY, s_xsrc)

            @block.vector
            def _(dve):
                seg = Segments(dve)
                segbox.append(seg)
                ch = seg.ch
                ch.link(nc.vector.memset(lg[:, :], 1.0))
                seg.total(run[:, :], lg[:, :])
                nc.vector.tensor_scalar(lg[:, :], run[:, :], 1.0, None, ALU.max).then_inc(s_degm, 1)
                dve.wait_ge(s_degr, 1)
                ch.link(nc.vector.reciprocal(mx[:, :], ls[:, :]))
                nc.vector.tensor_copy(INFO[:, :, 1], mx[:, :]).then_inc(s_deg, 1)
                seg.spread(isq[:, :], mx[:, :], tmp[:, :])
                ch.link(nc.vector.reciprocal(mx[:, :], lg[:, :]))
                for g in range(EG):
                    dve.wait_ge(s_aep, g + 1)
                    nc.vector.tensor_copy(AE[:, g * Q:(g + 1) * Q, :],
                                          PZ[g % 2][0:P, 0, 0:Q * L].rearrange("p (a l) -> p a l", a=Q)).then_inc(s_aes, 1)
                dve.wait_ge(s_aes, EG)
                for l in range(L):
                    ch.link(nc.vector.tensor_copy(ls[:, :], AE[:, :, l]))
                    seg.total(lg[:, :], ls[:, :])
                    ch.link(nc.vector.tensor_tensor(AL[:, :, l], lg[:, :], mx[:, :], ALU.mult))

            @block.tensor
            def _(pe):
                seg = segbox[0]
                carries(pe, seg, [("total", run[:, :]), ("spread", isq[:, :])])
                pe.wait_ge(s_ea, 32)
                for g in range(EG):
                    if g >= 2:
                        pe.wait_ge(s_eac, g - 1)
                    transposes(PT[g % 2], [R[:, 1 + g * Q + a, :] for a in range(Q)]).then_inc(s_eaT, 1)
                    pe.wait_ge(s_eac, g + 1)
                    if g >= 2:
                        pe.wait_ge(s_aes, g - 1)
                    for a in range(Q):
                        ins = nc.tensor.matmul(PZ[g % 2][0:P, 0, a * L:(a + 1) * L],
                                               XT[:, g % 2, a * P:(a + 1) * P], VE[:, :], start=True, stop=True)
                    ins.then_inc(s_aep, 1)
                for l in range(L):
                    pe.wait_ge(*seg.asked.at(3 + l))
                    nc.tensor.matmul(PZ[3][0:P, 0, 0:1], MF[:, :], lg[:, C - 1:C], start=True,
                                     stop=True).then_inc(seg.carried.s, 1)

            @block.scalar
            def _(act):
                act.wait_ge(s_degm, 1)
                nc.scalar.activation(ls[:, :], lg[:, :], ACT.Sqrt).then_inc(s_degr, 1)
                for g in range(EG):
                    act.wait_ge(s_eaT, g + 1)
                    if g >= 2:
                        act.wait_ge(s_aep, g - 1)
                    nc.scalar.activation(XT[:, g % 2, :], PT[g % 2][:, 0:Q * P], ACT.Copy).then_inc(s_eac, 1)

        segbox[0].end()

        def dense(first_round, rounds, moves, move, arrive):
            loaded = signal("x_loaded_0", "x_loaded_1")
            stored = signal("out_stored_0", "out_stored_1")
            (y_ready, y_part, scales_ready, beta_added, t_done, xt_ready, z_done, slope_ready, sq_ready,
             var_ready, rt_ready, out_ready) = signal(
                "rows_ready", "rows_ready_scalar", "scales_ready", "beta_added", "transposed", "xt_ready", "product_done", "slope_ready", "squares_ready",
                "variance_ready", "root_ready", "out_ready")
            summed = signal("last_squares_summed")
            STEPS = 2 + L - 1
            K = STEPS * DS
            ITEMS = K + DS

            chains = []

            with nc.Block() as block:
                @block.gpsimd
                def _(pool):
                    parts = rounds * DS
                    for n in range(parts):
                        i, s = divmod(n, DS)
                        move(pool, moves * n // parts, moves * (n + 1) // parts)
                        pool.wait_ge(*t_done.at(i * K + DS + s + 1))
                        xs = X[:, i % 2, s * Q:(s + 1) * Q, :]
                        nc.gpsimd.tensor_tensor(xs, xs, B3[:, :].unsqueeze(1).broadcast_to([P, Q, D]),
                                                ALU.add).then_inc(beta_added.s, 1)
                    for done, value in arrive:
                        pool.wait_ge(done, value)

                @block.sync
                def _(sp):
                    for i in range(rounds + 2):
                        if i >= 2:
                            sp.wait_ge(*out_ready.at((i - 1) * DS))
                            dma2(sp, out_v[first_round + i - 2], X[:, i % 2, :, :], stored[i % 2].s)
                            sp.wait_ge(*stored[i % 2].at(32 * (i // 2)))
                        if i < rounds:
                            dma2(sp, X[:, i % 2, :, :], x_v[first_round + i], loaded[i % 2].s)

                @block.tensor
                def _(pe):
                    def product(i, n):
                        k, s = divmod(n, DS)
                        pe.wait_ge(*xt_ready.at(i * K + (n + 1)))
                        w, bias = (W0[:, :], L) if k == 0 else (WC[:, k - 1, :], k - 1)
                        products(DPZ[s], XT[:, n % 4, :], w, bias).then_inc(z_done.s, 1)

                    def turn(i, b):
                        for n in range(ITEMS):
                            if 0 <= n - 2 < K:
                                product(i, n - 2)
                            if n < K:
                                pe.wait_ge(*y_ready.at(i * K + (n + 1)))
                                if n < 2 * DS:
                                    pe.wait_ge(*y_part.at(i * (2 * DS) + (n + 1)))
                                s = n % DS
                                transposes(DPT[n % 3], [Y[:, s, a, :] for a in range(Q)]).then_inc(t_done.s, 1)
                    pairs(pe, rounds, turn)

                @block.scalar
                def _(act):
                    def root(i, n):
                        k, s = divmod(n, DS)
                        if k == STEPS:
                            act.wait_ge(*summed.at(i * DS + (s + 1)))
                        else:
                            act.wait_ge(*var_ready.at(i * K + (n + 1)))
                        roots(mv[:, s, :, 1] if k < 2 else ss[:, s, :], s).then_inc(rt_ready.s, 1)

                    def copy_transposed(i, n):
                        k, s = divmod(n, DS)
                        act.wait_ge(*t_done.at(i * K + (n + 1)))
                        if k < 2:
                            ins = nc.scalar.activation(XT[:, n % 4, :], DPT[n % 3][:, 0:Q * P], ACT.Relu)
                        else:
                            ins = nc.scalar.activation(XT[:, n % 4, :], DPT[n % 3][:, 0:Q * P], ACT.Identity,
                                                       bias=BC[:, k - 2:k - 1], scale=GC[:, k - 2:k - 1])
                        ins.then_inc(xt_ready.s, 1)

                    def square(i, n):
                        k, s = divmod(n, DS)
                        act.wait_ge(*z_done.at(i * K + (n + 1)))
                        if k == 0:
                            nc.scalar.mul(Y[:, s, :, :], DPZ[s][0:P, :, :], 0.01).then_inc(slope_ready.s, 1)
                        elif k == STEPS - 1:
                            for a in range(Q):
                                ins = nc.scalar.activation(Y[:, s, a, :], DPZ[s][0:P, a, :], ACT.Square,
                                                           scale=D ** -0.5, accum_out=ss[:, s, a:a + 1])
                            ins.then_inc(summed.s, 1)
                        else:
                            nc.scalar.activation(Y[:, s, :, :], DPZ[s][0:P, :, :], ACT.Square,
                                                 scale=D ** -0.5).then_inc(sq_ready.s, 1)

                    def normalise_part(i, b, n):
                        k, s = divmod(n, DS)
                        act.wait_ge(*scales_ready.at(i * (2 * DS) + (n + 1)))
                        for a in range(ACT_TILES[k]):
                            ins = nc.scalar.activation(Y[:, s, a, :], X[:, b, s * Q + a, :], ACT.Identity,
                                                       bias=nm[:, s, a:a + 1], scale=rr[:, s, a:a + 1])
                        ins.then_inc(y_part.s, 1)

                    def turn(i, b):
                        root(i, 0)
                        for n in range(ITEMS):
                            if n + 1 < ITEMS:
                                root(i, n + 1)
                            if 0 <= n - 3 < K:
                                square(i, n - 3)
                            if 0 <= n - 1 < K:
                                copy_transposed(i, n - 1)
                            if n < 2 * DS:
                                normalise_part(i, b, n)
                    pairs(act, rounds, turn)

                @block.vector
                def _(dve):
                    per = DS * (2 * LN_LINKS + 2 + L + Q)
                    chains.append(Chain(dve, "dense_chain", per))
                    ch = chains[0]

                    def turn(i, b):
                        ch.turn(i)
                        dve.wait_ge(*loaded[b].at((i - b) * 16 + 32))

                        def cols_of(s):
                            return X[:, b, s * Q:(s + 1) * Q, :]

                        def measure(n):
                            k, s = divmod(n, DS)
                            if k == 0:
                                row_stats(ch, cols_of(s), s, var_ready.s)
                            elif k == 1:
                                dve.wait_ge(*slope_ready.at(i * DS + (s + 1)))
                                ch.link(nc.vector.tensor_tensor(Y[:, s, :, :], Y[:, s, :, :], DPZ[s][0:P, :, :],
                                                                ALU.max))
                                ch.link(nc.vector.tensor_tensor(cols_of(s), cols_of(s), Y[:, s, :, :], ALU.add))
                                row_stats(ch, cols_of(s), s, var_ready.s)
                            elif k < STEPS:
                                dve.wait_ge(*sq_ready.at(i * ((L - 1) * DS) + (n - 2 * DS + 1)))
                                nc.vector.tensor_reduce(ss[:, s, :], Y[:, s, :, :], AX.X,
                                                        ALU.add).then_inc(var_ready.s, 1)

                        def normalise(n):
                            k, s = divmod(n, DS)
                            dve.wait_ge(*rt_ready.at(i * ITEMS + (n + 1)))
                            if k < 2:
                                row_scales(ch, s, scales_ready.s)
                                dve.wait_ge(*scales_ready.at(i * (2 * DS) + (n + 1)))
                                for a in range(ACT_TILES[k], Q):
                                    ins = nc.vector.tensor_scalar(
                                        Y[:, s, a, :], cols_of(s)[:, a, :], rr[:, s, a:a + 1], nm[:, s, a:a + 1],
                                        ALU.mult, ALU.add)
                                ins.then_inc(y_ready.s, 1)
                                return
                            ch.link(nc.vector.reciprocal(rr[:, s, :], rt[:, s, :]))
                            if k < STEPS:
                                nc.vector.tensor_tensor(Y[:, s, :, :], DPZ[s][0:P, :, :],
                                                        wide(rr[:, s, :]), ALU.mult).then_inc(y_ready.s, 1)
                                return
                            for a in range(Q):
                                ch.add(nc.vector.scalar_tensor_tensor(
                                    Y[:, s, a, :], DPZ[s][0:P, a, :], rr[:, s, a:a + 1], G3[:, :],
                                    ALU.mult, ALU.mult))
                            ch.wait()
                            dve.wait_ge(*beta_added.at(i * DS + (s + 1)))
                            nc.vector.tensor_tensor(cols_of(s), cols_of(s), Y[:, s, :, :],
                                                    ALU.add).then_inc(out_ready.s, 1)

                        measure(0)
                        measure(1)
                        for n in range(ITEMS):
                            normalise(n)
                            if n + 2 < ITEMS:
                                measure(n + 2)
                        assert ch.n == per
                    pairs(dve, rounds, turn)

            chains[0].end(chains[0].per * rounds)
            for sig, each in ((y_ready, K), (t_done, K), (xt_ready, K), (z_done, K), (slope_ready, DS),
                              (y_part, 2 * DS), (scales_ready, 2 * DS), (beta_added, DS), (summed, DS),
                              (sq_ready, (L - 1) * DS), (var_ready, K), (rt_ready, ITEMS), (out_ready, DS)):
                sig.base += each * rounds
            for b in range(2):
                loaded[b].base += 32 * ((rounds - b + 1) // 2)
                stored[b].base += 32 * ((rounds - b + 1) // 2)

        def turns(eng, full, ns_full, ns_last, turn, unrolled=False):
            if unrolled:
                for i in range(full):
                    turn(i, ns_full)
            else:
                with eng.Fori(0, full) as i:
                    turn(i, ns_full)
            turn(full, ns_last)

        def group(buf, i, per, s, shift=0):
            if isinstance(i, int):
                c = i * per + s * Q + shift
                return buf[:, c:c + Q]
            return buf[:, bass.ds(i * per + (s * Q + shift), Q)]

        def column(buf, i, per, c):
            if isinstance(i, int):
                return buf[:, i * per + c]
            v = buf[:, bass.ds(i * per + c, 1)]
            return v.rearrange("p a f -> p (a f)") if len(v.shape) == 3 else v

        def scalar_of(buf, i, per, c):
            return buf[:, i * per + c:i * per + c + 1] if isinstance(i, int) else buf[:, bass.ds(i * per + c, 1)]

        W4 = NS * Q
        FULL4, LAST4 = C // W4, C % W4 // Q

        def run_columns(ch, i, s):
            for a in range(Q):
                c = s * Q + a
                ch.link(nc.vector.scalar_tensor_tensor(
                    column(R, i, W4, c + 1), column(R, i, W4, c), scalar_of(keep, i, W4, c),
                    column(R, i, W4, c + 1), ALU.mult, ALU.add))

        def carry_in():
            brought = signal("carry_product")
            with nc.Block() as block:
                @block.tensor
                def _(pe):
                    nc.tensor.matmul(PZ[0][0:P, 0, :], MF[:, :], R[:, C, :], start=True, stop=True).then_inc(brought.s, 1)

                @block.scalar
                def _(act):
                    act.wait_ge(*brought.at(1))
                    nc.scalar.activation(CAR[:, :], PZ[0][0:P, 0, :], ACT.Copy)
            brought.base += 1

        s_iscat = sem("info_scattered")
        s_igat = sem("info_gathered")

        def first_moves(pool, a, b):
            for m in range(a + XSRC_EARLY, b + XSRC_EARLY):
                step, c = divmod(m, C)
                if step == 0:
                    gather_x(pool, S, srcI, c, c + 1, s_xsrc)
                elif step == 1:
                    scatter(pool, info_t, repI[:, c:c + 1], N, INFO[:, c, :], s_iscat)
                elif step == 2:
                    gather_x(pool, T, dstI, c, c + 1, s_xdst)
                else:
                    if c == 0:
                        pool.wait_ge(s_iscat, 16 * C)
                    gather(pool, INFG[:, c, :], srcI[:, c:c + 1], info_t, N, s_igat)

        dense(0, SHARES[0], 4 * C - XSRC_EARLY, first_moves,
              [(s_xsrc, 16 * C), (s_xdst, 16 * C), (s_igat, 16 * C)])

        s_alpha = sem("conv_alpha_ready")
        y_ready, t_done, xt_ready, z_done, m_ready, biased, slope_ready, s_ready, var_ready, rt_ready = (
            sem("convS_" + n) for n in ("rows_ready", "transposed", "xt_ready", "product_done",
                                        "message_ready", "bias_added", "slope_ready", "rows_final",
                                        "variance_ready", "root_ready"))
        with nc.Block() as block:
            @block.tensor
            def _(pe):
                def turn(i, ns):
                    for s in range(ns):
                        pe.wait_ge(y_ready, i * NS + (s + 1))
                        transposes(PT[s], [Y[:, s, a, :] for a in range(Q)]).then_inc(t_done, 1)
                    for s in range(ns):
                        pe.wait_ge(xt_ready, i * NS + (s + 1))
                        products(PZ[s], XT[:, s, :], W0[:, :], None).then_inc(z_done, 1)
                    for s in range(ns):
                        pe.wait_ge(m_ready, i * NS + (s + 1))
                        nc.tensor.matmul(PZ[s][0:P, :, :], ones3[:, 0:P], BR[:, L:L + 1, :].broadcast_to([3, Q, D]),
                                         start=False, stop=True, skip_group_check=True).then_inc(biased, 1)
                turns(pe, FULL4, NS, LAST4, turn)

            @block.scalar
            def _(act):
                act.wait_ge(s_alpha, 1)

                def turn(i, ns):
                    for s in range(ns):
                        act.wait_ge(var_ready, i * 2 * NS + (s + 1))
                        roots(mv[:, s, :, 1], s).then_inc(rt_ready, 1)
                    for s in range(ns):
                        act.wait_ge(t_done, i * NS + (s + 1))
                        nc.scalar.activation(XT[:, s, :], PT[s][:, 0:Q * P], ACT.Relu).then_inc(xt_ready, 1)
                    for s in range(ns):
                        act.wait_ge(z_done, i * NS + (s + 1))
                        for a in range(Q):
                            ins = nc.scalar.activation(column(R, i, W4, s * Q + a + 1), PZ[s][0:P, a, :], ACT.Copy,
                                                       scale=scalar_of(alpha, i, W4, s * Q + a))
                        ins.then_inc(m_ready, 1)
                    for s in range(ns):
                        act.wait_ge(biased, i * NS + (s + 1))
                        nc.scalar.mul(Y[:, s, :, :], PZ[s][0:P, :, :], 0.01).then_inc(slope_ready, 1)
                    for s in range(ns):
                        act.wait_ge(var_ready, i * 2 * NS + (ns + s + 1))
                        roots(mv[:, s, :, 1], s).then_inc(rt_ready, 1)
                turns(act, FULL4, NS, LAST4, turn)

            @block.vector
            def _(dve):
                c0 = Chain(dve, "convS_alpha_chain")
                c0.link(nc.vector.tensor_tensor(alpha[:, :], isq[:, :], wE[:, :], ALU.mult))
                nc.vector.tensor_tensor(alpha[:, :], alpha[:, :], INFG[:, :, 1], ALU.mult).then_inc(s_alpha, 1)
                ch = Chain(dve, "convS_chain", NS * (2 * LN_LINKS + 2 + Q))

                def turn(i, ns):
                    ch.turn(i)
                    for s in range(ns):
                        row_stats(ch, group(S, i, W4, s), s, var_ready)
                    for s in range(ns):
                        dve.wait_ge(rt_ready, i * 2 * NS + (s + 1))
                        row_normal(ch, group(S, i, W4, s), Y[:, s, :, :], s, y_ready)
                    for s in range(ns):
                        dve.wait_ge(m_ready, i * NS + (s + 1))
                        run_columns(ch, i, s)
                    for s in range(ns):
                        dve.wait_ge(slope_ready, i * NS + (s + 1))
                        sg = group(S, i, W4, s)
                        ch.link(nc.vector.tensor_tensor(Y[:, s, :, :], Y[:, s, :, :], PZ[s][0:P, :, :], ALU.max))
                        ch.link(nc.vector.tensor_tensor(sg, sg, Y[:, s, :, :], ALU.add))
                        row_stats(ch, sg, s, var_ready)
                    for s in range(ns):
                        dve.wait_ge(rt_ready, i * 2 * NS + (ns + s + 1))
                        sg = group(S, i, W4, s)
                        row_normal(ch, sg, sg, s, s_ready)
                turns(dve, FULL4, NS, LAST4, turn)

        carry_in()

        y_ready2, t_done2, xt_ready2, z_done2, x1_ready, t_ready, var_ready2, rt_ready2 = (
            sem("convT_" + n) for n in ("rows_ready", "transposed", "xt_ready", "product_done",
                                        "x1_ready", "rows_final",
                                        "variance_ready", "root_ready"))
        s_x1 = sem("x1_stored")
        s_rows = sem("rows_stored")

        with nc.Block() as block:
            @block.sync
            def _(sp):
                for i in range(FULL4 + 1):
                    c0, c1 = i * W4, min(C, (i + 1) * W4)
                    sp.wait_ge(x1_ready, c1 // Q)
                    dma2(sp, x1_v[:, c0:c1, :], R[:, c0 + 1:c1 + 1, :], s_x1)
                    sp.wait_ge(t_ready, c1 // Q)
                    dma2(sp, row_v[:, c0:c1, :], T[:, c0:c1, :], s_rows)
                sp.wait_ge(s_x1, 32 * (FULL4 + 1))
                sp.wait_ge(s_rows, 32 * (FULL4 + 1))

            @block.tensor
            def _(pe):
                def turn(i, ns):
                    for s in range(ns):
                        pe.wait_ge(y_ready2, i * NS + (s + 1))
                        transposes(PT[s], [Y[:, s, a, :] for a in range(Q)]).then_inc(t_done2, 1)
                    for s in range(ns):
                        pe.wait_ge(xt_ready2, i * NS + (s + 1))
                        products(PZ[s], XT[:, s, :], W0[:, :], L).then_inc(z_done2, 1)
                turns(pe, FULL4, NS, LAST4, turn)

            @block.scalar
            def _(act):
                def turn(i, ns):
                    for s in range(ns):
                        act.wait_ge(var_ready2, i * 2 * NS + (s + 1))
                        roots(mv[:, s, :, 1], s).then_inc(rt_ready2, 1)
                    for s in range(ns):
                        act.wait_ge(t_done2, i * NS + (s + 1))
                        nc.scalar.activation(XT[:, s, :], PT[s][:, 0:Q * P], ACT.Relu).then_inc(xt_ready2, 1)
                    for s in range(ns):
                        act.wait_ge(var_ready2, i * 2 * NS + (ns + s + 1))
                        roots(mv[:, s, :, 1], s).then_inc(rt_ready2, 1)
                turns(act, FULL4, NS, LAST4, turn)

            @block.vector
            def _(dve):
                ch = Chain(dve, "convT_chain", NS * (2 * LN_LINKS + Q + 2))

                def turn(i, ns):
                    ch.turn(i)
                    for s in range(ns):
                        row_stats(ch, group(T, i, W4, s), s, var_ready2)
                    for s in range(ns):
                        dve.wait_ge(rt_ready2, i * 2 * NS + (s + 1))
                        row_normal(ch, group(T, i, W4, s), Y[:, s, :, :], s, y_ready2)
                    for s in range(ns):
                        for a in range(Q):
                            c = s * Q + a
                            ch.add(nc.vector.scalar_tensor_tensor(
                                column(R, i, W4, c + 1), CAR[:, :], scalar_of(first, i, W4, c),
                                column(R, i, W4, c + 1), ALU.mult, ALU.add))
                        ch.wait()
                        dve.wait_ge(z_done2, i * NS + (s + 1))
                        rg = group(R, i, W4, s, 1)
                        tg = group(T, i, W4, s)
                        ch.link(nc.vector.tensor_tensor(rg, rg, PZ[s][0:P, :, :], ALU.add))
                        ch.link(leaky(Y[:, s, :, :], rg, 0.01))
                        nc.vector.tensor_tensor(rg, tg, Y[:, s, :, :], ALU.add).then_inc(x1_ready, 1)
                        dve.wait_ge(x1_ready, i * NS + (s + 1))
                        row_stats(ch, rg, s, var_ready2)
                    for s in range(ns):
                        dve.wait_ge(rt_ready2, i * 2 * NS + (ns + s + 1))
                        row_normal(ch, group(R, i, W4, s, 1), group(T, i, W4, s), s, t_ready)
                turns(dve, FULL4, NS, LAST4, turn)

        s_refresh = sem("s_refreshed")

        def refresh(pool, a, b):
            for c in range(a, b):
                gather(pool, S[:, c, :], INFG[:, c, 0:1].bitcast(I32), row_t, E, s_refresh)

        W2 = 2 * Q
        FULL2 = C // W2
        s_x1b = sem("x1_loaded")
        s_out = sem("out_scattered")

        def attention(l):
            final = l == L - 1

            t_done, xt_ready, z_done, sq_ready, var_ready, rt_ready, copied, scaled = signal(
                "transposed", "xt_ready", "product_done", "squares_ready", "variance_ready", "root_ready",
                "message_copied", "rows_scaled")
            chains = []
            with nc.Block() as block:
                def streams(ns):
                    return range(NS) if ns == NS else (0, 2)

                def order(i, n):
                    return i * NS + (n + 1)

                @block.tensor
                def _(pe):
                    def turn(i, ns):
                        for n, s in enumerate(streams(ns)):
                            buf, g = (S, s) if s < 2 else (T, s - 2)
                            if i:
                                pe.wait_ge(*scaled.at(order(i - 1, s)))
                            c = i * W2 + g * Q
                            transposes(PT[s], [buf[:, c + a, :] for a in range(Q)]).then_inc(t_done.s, 1)
                        for n, s in enumerate(streams(ns)):
                            pe.wait_ge(*xt_ready.at(order(i, n)))
                            if s < 2 and i:
                                pe.wait_ge(*copied.at((i - 1) * 2 + s + 1))
                            for a in range(Q):
                                nc.tensor.matmul(PT[s][0:P, 500 + 2 * a:502 + 2 * a], XT[:, s, a * P:(a + 1) * P],
                                                 SD[:, l, :], start=True, stop=True, skip_group_check=True)
                            products(PZ[s], XT[:, s, :], WC[:, l, :], l).then_inc(z_done.s, 1)
                    turns(pe, FULL2, NS, 2, turn, unrolled=True)

                @block.scalar
                def _(act):
                    def turn(i, ns):
                        for n, s in enumerate(streams(ns)):
                            act.wait_ge(*t_done.at(order(i, n)))
                            if l == 0:
                                ins = nc.scalar.activation(XT[:, s, :], PT[s][:, 0:Q * P], ACT.Relu)
                            else:
                                ins = nc.scalar.activation(XT[:, s, :], PT[s][:, 0:Q * P], ACT.Identity,
                                                           bias=BC[:, l - 1:l], scale=GC[:, l - 1:l])
                            ins.then_inc(xt_ready.s, 1)
                        for n, s in enumerate(streams(ns)):
                            if s >= 2:
                                continue
                            act.wait_ge(*z_done.at(order(i, n)))
                            if not final:
                                nc.scalar.activation(Y[:, s, :, :], PZ[s][0:P, :, :], ACT.Square,
                                                     scale=D ** -0.5).then_inc(sq_ready.s, 1)
                            nc.scalar.activation(group(R, i, W2, s, 1), PZ[s][0:P, :, :],
                                                 ACT.Copy).then_inc(copied.s, 1)
                            if not final:
                                act.wait_ge(*var_ready.at(i * 2 + (n + 1)))
                                roots(ss[:, s, :], s).then_inc(rt_ready.s, 1)
                    turns(act, FULL2, NS, 2, turn)

                @block.vector
                def _(dve):
                    ch = Chain(dve, "project_chain", 2 if final else 6)
                    chains.append(ch)

                    def turn(i, ns):
                        ch.turn(i)
                        for n, s in enumerate(streams(ns)):
                            dve.wait_ge(*z_done.at(order(i, n)))
                            sc, g = (SCS, s) if s < 2 else (SCT, s - 2)
                            ins = nc.vector.tensor_copy(group(sc, i, W2, g), PT[s][0:P, 500:508]
                                                        .rearrange("p (a k) -> p a k", k=2))
                            if s >= 2:
                                ch.add(ins)
                                nc.vector.tensor_copy(group(T, i, W2, g), PZ[s][0:P, :, :]).then_inc(scaled.s, 1)
                            elif final:
                                ins.then_inc(scaled.s, 1)
                            else:
                                ch.add(ins)
                                dve.wait_ge(*sq_ready.at(i * 2 + (n + 1)))
                                nc.vector.tensor_reduce(ss[:, s, :], Y[:, s, :, :], AX.X,
                                                        ALU.add).then_inc(var_ready.s, 1)
                                dve.wait_ge(*rt_ready.at(i * 2 + (n + 1)))
                                ch.link(nc.vector.reciprocal(rr[:, s, :], rt[:, s, :]))
                                nc.vector.tensor_tensor(group(S, i, W2, g), PZ[s][0:P, :, :], wide(rr[:, s, :]),
                                                        ALU.mult).then_inc(scaled.s, 1)
                    turns(dve, FULL2, NS, 2, turn)

            chains[0].end()
            for sig in (t_done, xt_ready, z_done, scaled):
                sig.base += 2 * C // Q
            copied.base += C // Q
            for sig in (sq_ready, var_ready, rt_ready):
                sig.base += 0 if final else C // Q

            act_in, act_out = signal("exponents_ready", "exp_done")
            segbox = []
            with nc.Block() as block:
                @block.vector
                def _(dve):
                    seg = Segments(dve)
                    segbox.append(seg)
                    ch = seg.ch

                    def op(o, a, b, f):
                        ch.link(nc.vector.tensor_tensor(o[:, :], a, b, f))

                    seg.spread(run[:, :], SCT[:, :, 1], tmp[:, :])
                    op(lg, SCS[:, :, 0], run[:, :], ALU.add)
                    op(lg, lg[:, :], AE[:, :, l], ALU.add)
                    ch.link(nc.vector.scalar_tensor_tensor(lg[:, :], lg[:, :], 0.2, lg[:, :], ALU.mult, ALU.max))
                    op(ls, SCT[:, :, 0], SCT[:, :, 1], ALU.add)
                    op(ls, ls[:, :], AL[:, :, l], ALU.add)
                    ch.link(nc.vector.scalar_tensor_tensor(ls[:, :], ls[:, :], 0.2, ls[:, :], ALU.mult, ALU.max))
                    seg.maximum(mx[:, :], lg[:, :])
                    op(mx, mx[:, :], ls[:, :], ALU.max)
                    seg.spread(run[:, :], mx[:, :], tmp[:, :])
                    op(lg, lg[:, :], run[:, :], ALU.subtract)
                    op(ls, ls[:, :], run[:, :], ALU.subtract)
                    nc.vector.tensor_scalar(ls[:, :], ls[:, :], 0.0, None, ALU.min).then_inc(act_in.s, 1)
                    dve.wait_ge(*act_out.at(2))
                    seg.total(run[:, :], alpha[:, :])
                    op(run, run[:, :], aself[:, :], ALU.add)
                    ch.link(nc.vector.tensor_scalar(run[:, :], run[:, :], 1e-16, None, ALU.add))
                    seg.spread(mx[:, :], run[:, :], tmp[:, :])
                    ch.link(nc.vector.reciprocal(mx[:, :], mx[:, :]))
                    op(alpha, alpha[:, :], mx[:, :], ALU.mult)
                    op(aself, aself[:, :], mx[:, :], ALU.mult)

                @block.tensor
                def _(pe):
                    carries(pe, segbox[0], [("spread", run[:, :]), ("max", None), ("spread", run[:, :]),
                                            ("total", run[:, :]), ("spread", mx[:, :])])

                @block.scalar
                def _(act):
                    act.wait_ge(*act_in.at(1))
                    nc.scalar.activation(alpha[:, :], lg[:, :], ACT.Exp).then_inc(act_out.s, 1)
                    nc.scalar.activation(aself[:, :], ls[:, :], ACT.Exp).then_inc(act_out.s, 1)

                @block.sync
                def _(sp):
                    if final:
                        dma2(sp, S, x1_v, s_x1b)
                        sp.wait_ge(s_x1b, 32)

            segbox[0].end()
            act_in.base += 1
            act_out.base += 2
            weighted = signal("messages_weighted")
            with nc.Block() as block:
                @block.scalar
                def _(act):
                    def turn(i, ns):
                        for s in range(ns):
                            for a in range(Q):
                                c = s * Q + a
                                ins = nc.scalar.activation(column(R, i, W4, c + 1), column(R, i, W4, c + 1), ACT.Copy,
                                                           scale=scalar_of(alpha, i, W4, c))
                            ins.then_inc(weighted.s, 1)
                    turns(act, FULL4, NS, LAST4, turn)

                @block.vector
                def _(dve):
                    ch = Chain(dve, "run_chain", NS * Q)
                    chains.append(ch)

                    def turn(i, ns):
                        ch.turn(i)
                        for s in range(ns):
                            dve.wait_ge(*weighted.at(i * NS + (s + 1)))
                            run_columns(ch, i, s)
                    turns(dve, FULL4, NS, LAST4, turn)

            carry_in()

            chains[1].end()
            weighted.base += C // Q

            sum_ready, sq_ready2, var_ready2, rt_ready2, t_ready = signal(
                "sum_ready", "squares_ready", "variance_ready", "root_ready", "t_rows_final")
            with nc.Block() as block:
                @block.vector
                def _(dve):
                    ch = Chain(dve, "t_chain", NS * (Q + 1 + (Q + 1 if final else 0)))
                    chains.append(ch)

                    def turn(i, ns):
                        ch.turn(i)
                        for s in range(ns):
                            for a in range(Q):
                                c = s * Q + a
                                ch.add(nc.vector.scalar_tensor_tensor(
                                    column(T, i, W4, c), column(T, i, W4, c), scalar_of(aself, i, W4, c),
                                    column(R, i, W4, c + 1), ALU.mult, ALU.add))
                            ch.wait()
                            for a in range(Q):
                                c = s * Q + a
                                ins = nc.vector.scalar_tensor_tensor(
                                    column(T, i, W4, c), CAR[:, :], scalar_of(first, i, W4, c),
                                    column(T, i, W4, c), ALU.mult, ALU.add)
                            ins.then_inc(sum_ready.s, 1)
                        for s in range(ns):
                            dve.wait_ge(*sq_ready2.at(i * NS + (s + 1)))
                            nc.vector.tensor_reduce(ss[:, s, :], Y[:, s, :, :], AX.X,
                                                    ALU.add).then_inc(var_ready2.s, 1)
                        for s in range(ns):
                            dve.wait_ge(*rt_ready2.at(i * NS + (s + 1)))
                            tg = group(T, i, W4, s)
                            ch.link(nc.vector.reciprocal(rr[:, s, :], rt[:, s, :]))
                            if not final:
                                nc.vector.tensor_tensor(tg, tg, wide(rr[:, s, :]), ALU.mult).then_inc(t_ready.s, 1)
                                continue
                            for a in range(Q):
                                c = s * Q + a
                                ch.add(nc.vector.scalar_tensor_tensor(
                                    column(T, i, W4, c), column(T, i, W4, c), rr[:, s, a:a + 1], G3[:, :],
                                    ALU.mult, ALU.mult))
                            ch.wait()
                            ch.link(nc.vector.tensor_tensor(tg, tg, B3[:, :].unsqueeze(1).broadcast_to([P, Q, D]),
                                                            ALU.add))
                            nc.vector.tensor_tensor(tg, tg, group(S, i, W4, s), ALU.add).then_inc(t_ready.s, 1)
                    turns(dve, FULL4, NS, LAST4, turn)

                @block.scalar
                def _(act):
                    def turn(i, ns):
                        for s in range(ns):
                            act.wait_ge(*sum_ready.at(i * NS + (s + 1)))
                            nc.scalar.activation(Y[:, s, :, :], group(T, i, W4, s), ACT.Square,
                                                 scale=D ** -0.5).then_inc(sq_ready2.s, 1)
                        for s in range(ns):
                            act.wait_ge(*var_ready2.at(i * NS + (s + 1)))
                            roots(ss[:, s, :], s).then_inc(rt_ready2.s, 1)
                    turns(act, FULL4, NS, LAST4, turn)

                if final:
                    @block.gpsimd
                    def _(pool):
                        for c in range(C):
                            pool.wait_ge(*t_ready.at(c // Q + 1))
                            scatter(pool, out, repI[:, c:c + 1], N, T[:, c, :], s_out)
                        pool.wait_ge(s_out, 16 * C)
                else:
                    @block.sync
                    def _(sp):
                        before = 32 * (FULL4 + 1) * (l + 1)
                        for i in range(FULL4 + 1):
                            c0, c1 = i * W4, min(C, (i + 1) * W4)
                            sp.wait_ge(*t_ready.at(c1 // Q))
                            dma2(sp, row_v[:, c0:c1, :], T[:, c0:c1, :], s_rows)
                        sp.wait_ge(s_rows, before + 32 * (FULL4 + 1))

            chains[2].end()
            for sig in (sum_ready, sq_ready2, var_ready2, rt_ready2, t_ready):
                sig.base += C // Q

        done = SHARES[0]
        for l in range(L):
            dense(done, SHARES[l + 1], C, refresh, [(s_refresh, 16 * C * (l + 1))])
            done += SHARES[l + 1]
            attention(l)
        assert done == ROUNDS


_INS = ["x", "src", "dst", "edge_attr_128", "edge_weight", "L0_gnn_W_weight", "L0_gnn_W_bias", "L1_gnn_W",
        "L1_gnn_We", "L1_gnn_att_src", "L1_gnn_att_dst", "L1_gnn_att_edge", "L1_gnn_bias",
        "L1_gnn_ln_gamma", "L1_gnn_ln_beta"]


def kernel(**inputs):
    import numpy as np
    import concourse.bacc as bacc
    from concourse.bass_utils import run_bass_kernel_spmd

    nc = bacc.Bacc("TRN2", target_bir_lowering=False, num_devices=1)
    arrays, args = {}, []
    for name in _INS:
        a = np.ascontiguousarray(inputs[name])
        arrays["in_" + name] = a
        args.append(nc.dram_tensor("in_" + name, a.shape, mybir.dt.from_np(a.dtype), kind="ExternalInput").ap())
    out = nc.dram_tensor("out_rows", (N, D), F32, kind="ExternalOutput").ap()
    gnn_kernel(nc, *args, out)
    r = run_bass_kernel_spmd(nc, [arrays], core_ids=[0])
    return r.results[0]["out_rows"]
```

```python
import concourse.bass as bass
from concourse import mybir
from contextlib import ExitStack

F32 = mybir.dt.float32
I32 = mybir.dt.int32
BF16 = mybir.dt.bfloat16
ALU = mybir.AluOpType
ACT = mybir.ActivationFunctionType
AX = mybir.AxisListType

D = 128
N = 50000
E = 12500
L = 4
P = 125
C = E // P
Q = 4
NS = 4
HALF = C // Q // 2
DS = 5
ROUND = P * DS * Q
ROUNDS = N // ROUND
SW = 64
CORE = 112
EPS = 1e-5
BIG = 1e30
NOWHERE = 1 << 23
SHARES = [8, 3, 3, 3, 3]


def gnn_kernel(nc, x, src, dst, ea, ew, w0, b0, wg, we, att_s, att_d, att_e, bg, gamma, beta, out):
    ctx = ExitStack()
    with ctx:
        ctx.enter_context(nc.allow_non_contiguous_dma(reason="a few hundred single elements, once"))

        def sb(name, shape, dt=F32):
            return ctx.enter_context(nc.sbuf_tensor(name, shape, dt))

        def sem(name):
            return ctx.enter_context(nc.semaphore(name))

        class Signal:

            def __init__(self, name):
                self.s, self.base = sem(name), 0

            def at(self, n):
                return self.s, self.base + n

        signals = {}

        def signal(*names):
            for n in names:
                if n not in signals:
                    signals[n] = Signal(n)
            got = [signals[n] for n in names]
            return got if len(got) > 1 else got[0]

        S = sb("S", [P, C, D])
        T = sb("T", [P, C, D])
        R = sb("R", [P, C + 1, D])
        X = R[:, 1:1 + 2 * DS * Q, :].rearrange("p (b r) f -> p b r f", b=2)
        YB = sb("Y", [D, DS, Q, D])
        Y = YB[0:P, :, :, :]
        XT = sb("XT", [D, NS, Q * P])
        ident = sb("ident", [D, D])
        ones = sb("ones", [D, D])
        ones3 = sb("ones3", [3, D], BF16)
        W0 = sb("W0", [D, D])
        WC = sb("WC", [D, L, D])
        SD = sb("SD", [D, L, SW])
        VE = sb("VE", [D, L])
        BR = sb("BR", [3, L + 1, D], BF16)
        GC = sb("GC", [D, L])
        BC = sb("BC", [D, L])
        G3 = sb("G3", [P, D])
        B3 = sb("B3", [P, D])
        B0 = sb("B0", [P, D])
        MF = sb("MF", [P, P])
        MB = sb("MB", [P, P])
        PM = sb("PM", [P, P])
        DG = sb("DG", [P, P])
        CAR = sb("CAR", [P, D])
        CAR2 = sb("CAR2", [P, D])
        END = sb("END", [P, D])

        def cols(name, dt=F32):
            return sb(name, [P, C], dt)

        keep, knext, rep, first, last, pen, penf, cont = (cols(n) for n in (
            "keep", "knext", "rep", "first", "last", "pen", "penf", "cont"))
        srcI, dstI, repI = (cols(n, I32) for n in ("srcI", "dstI", "repI"))
        wE, lg, ls, run, mx, tmp, alpha, aself, isq = (cols(n) for n in (
            "wE", "lg", "ls", "run", "mx", "tmp", "alpha", "aself", "isq"))
        AE = sb("AE", [P, C, L])
        AL = sb("AL", [P, C, L])
        INFO = sb("INFO", [P, C, 2])
        INFG = sb("INFG", [P, C, 2])
        SCS = sb("SCS", [P, C, 2])
        SCT = sb("SCT", [P, C, 2])
        st = sb("st", [P, 4, Q, 6])
        mv = sb("mv", [P, DS, Q, 2])
        rt = sb("rt", [P, DS, Q])
        nm = sb("nm", [P, DS, Q])
        epsc = sb("epsc", [P, 1])
        taken = sb("taken", [P, 8])
        rr = sb("rr", [P, DS, Q])
        ss = sb("ss", [P, DS, Q])
        car1 = sb("car1", [P, L])

        banks = [ctx.enter_context(nc.psum_tensor(f"bank{b}", [D, 512], F32)) for b in range(8)]

        def tiles_of(bank):
            return bank[:, :].rearrange("p (a f) -> p a f", a=Q)

        PT, PZ = banks[0:4], [tiles_of(b) for b in banks[4:8]]
        DPT, DPZ = banks[0:3], [tiles_of(b) for b in banks[3:8]]

        info_t = nc.dram_tensor("info_t", [N, 2], F32, kind="Internal").ap()
        row_t = nc.dram_tensor("row_t", [E, D], F32, kind="Internal").ap()
        x1_t = nc.dram_tensor("x1_t", [E, D], F32, kind="Internal").ap()
        row_v = row_t.rearrange("(p c) f -> p c f", p=P)
        x1_v = x1_t.rearrange("(p c) f -> p c f", p=P)
        x_v = x.rearrange("(i p r) f -> i p r f", p=P, r=DS * Q)
        out_v = out.rearrange("(i p r) f -> i p r f", p=P, r=DS * Q)

        def dma2(eng, dst_ap, src_ap, s):
            eng.dma_start(dst_ap[0:CORE], src_ap[0:CORE]).then_inc(s, 16)
            eng.dma_start(dst_ap[CORE:P], src_ap[CORE:P]).then_inc(s, 16)

        class Chain:

            def __init__(self, dve, name, per=0):
                self.dve, self.done, self.per, self.n, self.base = dve, signal(name), per, 0, 0

            def turn(self, i):
                self.base, self.n = i * self.per, 0

            def add(self, ins):
                ins.then_inc(self.done.s, 1)
                self.n += 1

            def wait(self):
                self.dve.wait_ge(*self.done.at(self.base + self.n))

            def link(self, ins):
                self.add(ins)
                self.wait()

            def end(self, total=None):
                self.done.base += self.base + self.n if total is None else total

        def take_wait(n):
            nc.vector.memset(taken[:, n:n + 1], 0.0)

        ACT_TILES = (2, 3)

        def leaky(o, v, slope):
            return nc.vector.scalar_tensor_tensor(o, v, slope, v, ALU.mult, ALU.max)

        def roots(v, s):
            return nc.scalar.activation(rt[:, s, :], v, ACT.Sqrt, bias=epsc[:, 0:1])

        def wide(v, n=Q):
            return v.unsqueeze(2).broadcast_to([P, n, D])

        def transposes(ps, tiles):
            for a, t in enumerate(tiles):
                ins = nc.tensor.transpose(ps[:, a * P:(a + 1) * P], t, ident[0:P, 0:P])
            return ins

        def products(pz, xt, w, bias):
            if bias is not None:
                nc.tensor.matmul(pz[0:P, :, :], ones3[:, 0:P],
                                 BR[:, bias:bias + 1, :].broadcast_to([3, Q, D]),
                                 start=True, stop=False, skip_group_check=True)
            for a in range(Q):
                ins = nc.tensor.matmul(pz[0:P, a, :], xt[:, a * P:(a + 1) * P], w,
                                       start=bias is None and a == 0, stop=True, skip_group_check=True)
            return ins

        def gather(pool, to, idx, table, rows, done):
            pool.indirect_dma_start(to, None, table, bass.IndirectOffsetOnAxis(ap=idx, axis=0),
                                    bounds_check=rows - 1, oob_is_err=False).then_inc(done, 16)

        def scatter(pool, table, idx, rows, frm, done):
            pool.indirect_dma_start(table, bass.IndirectOffsetOnAxis(ap=idx, axis=0), frm, None,
                                    bounds_check=rows - 1, oob_is_err=False).then_inc(done, 16)

        def gather_x(pool, to, idx, c0, c1, done):
            for c in range(c0, c1):
                gather(pool, to[:, c, :], idx[:, c:c + 1], x, N, done)

        s_w = sem("weights_loaded")
        s_meta = sem("edges_loaded")
        s_halo = sem("halo_cleared")
        s_id = sem("identity_ready")
        s_bs = sem("bias_split")
        s_br = sem("bias_rows_placed")
        s_wT = sem("w0_transposed")
        s_diag = sem("diagonal_ready")
        s_bc = sem("row_broadcast")
        s_ea = sem("edge_attr_loaded")
        s_fill = sem("info_filled")
        s_filled = sem("info_table_filled")
        s_idx = sem("indices_loaded")
        s_xsrc = sem("x_src_gathered")
        s_xdst = sem("x_dst_gathered")

        wide0 = XT[:, :, :].rearrange("p s q -> p (s q)")
        WR = wide0[:, 0:L * D].rearrange("p (l f) -> p l f", l=L)
        WER = wide0[:, 512:512 + L * D].rearrange("p (l f) -> p l f", l=L)
        PR = wide0[:, 1024:1024 + L * D].rearrange("p (l f) -> p l f", l=L)
        W0R = wide0[:, 1536:1536 + D]
        rowm = wide0[:, 1664:1664 + L]
        Yb = YB[:, :, :, :].rearrange("p s q f -> p (s q f)")
        attb = Yb[:, 1408:1408 + L * D]
        Yf = Yb[0:P]
        DH = Yf[:, 0:C + 2].bitcast(I32)
        DF = Yf[:, 128:128 + C + 2]
        brow = Yf[0:1, 256:256 + (L + 1) * D].rearrange("p (l f) -> p l f", l=L + 1)
        blo = X[0:1, 1, 8:8 + L + 1, :]
        bm = Yf[0:1, 1000:1000 + L + 1]
        bpart = X[0:1, 1, 0:8, :].rearrange("p a f -> p (a f)")[:, 0:960].bitcast(BF16) \
            .rearrange("p (k l f) -> p k l f", k=3, l=L + 1)
        fill = X[:, 0, :, :].rearrange("p a f -> p (a f)")[:, 0:800].rearrange("p (n k) -> p n k", k=2)

        with nc.Block() as block:
            @block.sync
            def _(sp):
                for a, b in ((WR, wg.rearrange("l k j -> k l j")), (WER, we.rearrange("l k j -> k l j")),
                             (W0R, w0), (GC[:, :], gamma.rearrange("l f -> f l")),
                             (BC[:, :], beta.rearrange("l f -> f l")),
                             (brow[:, 0:L, :], bg.unsqueeze(0)), (brow[:, L, :], b0.unsqueeze(0)),
                             (G3[:, :], gamma[L - 1:L, :].broadcast_to([P, D])),
                             (B3[:, :], beta[L - 1:L, :].broadcast_to([P, D])),
                             (B0[:, :], b0.unsqueeze(0).broadcast_to([P, D]))):
                    sp.dma_start(a, b).then_inc(s_w, 16)
                dv = dst.rearrange("(p c) -> p c", p=P)
                sp.wait_ge(s_halo, 1)
                sp.dma_start(DH[:, 1:C + 1], dv).then_inc(s_meta, 16)
                sp.dma_start(DH[1:P, 0:1], dv[0:P - 1, C - 1:C]).then_inc(s_meta, 16)
                sp.dma_start(DH[0:P - 1, C + 1:C + 2], dv[1:P, 0:1]).then_inc(s_meta, 16)
                sp.dma_start(wE[:, :], ew.rearrange("(p c) -> p c", p=P)).then_inc(s_meta, 16)
                sp.dma_start(srcI[:, :], src.rearrange("(p c) -> p c", p=P)).then_inc(s_idx, 16)
                sp.dma_start(dstI[:, :], dv).then_inc(s_idx, 16)
                sp.wait_ge(s_bs, 1)
                for k in range(3):
                    sp.dma_start(BR[k:k + 1, :, :], bpart[:, k, :, :]).then_inc(s_br, 16)
                sp.wait_ge(s_br, 48)
                sp.wait_ge(s_fill, 1)
                dma2(sp, info_t.rearrange("(p n) k -> p n k", p=P), fill, s_filled)
                sp.wait_ge(s_filled, 32)
                dma2(sp, R[:, 1:C + 1, :], ea.rearrange("(p c) f -> p c f", p=P), s_ea)
                sp.wait_ge(s_filled, 32)
                sp.wait_ge(s_idx, 32)

            s_att = sem("att_loaded")
            s_attf = sem("att_used")

            @block.scalar
            def _(act):
                for n, att in enumerate((att_s, att_d, att_e)):
                    if n:
                        act.wait_ge(s_attf, n)
                    act.dma_start(attb[:, :], att.rearrange("l f -> (l f)").unsqueeze(0)
                                  .broadcast_to([D, L * D])).then_inc(s_att, 16)
                act.wait_ge(s_att, 48)

            @block.gpsimd
            def _(pool):
                z1 = sem("zeros_set")
                nc.gpsimd.memset(ident[:, :], 0.0).then_inc(z1, 1)
                nc.gpsimd.memset(ones[:, :], 1.0)
                nc.gpsimd.memset(ones3[:, :], 1.0)
                nc.gpsimd.memset(epsc[:, :], EPS)
                nc.gpsimd.memset(MF[:, :], 1.0).then_inc(z1, 1)
                nc.gpsimd.memset(MB[:, :], 1.0).then_inc(z1, 1)
                pool.wait_ge(z1, 3)
                nc.gpsimd.affine_select(out=ident[:, :], in_=ident[:, :], compare_op=ALU.not_equal,
                                        fill=1.0, base=0, pattern=[[-1, D]], channel_multiplier=1)
                nc.gpsimd.affine_select(out=MF[:, :], in_=MF[:, :], compare_op=ALU.is_gt, fill=0.0,
                                        base=0, pattern=[[1, P]], channel_multiplier=-1)
                nc.gpsimd.affine_select(out=MB[:, :], in_=MB[:, :], compare_op=ALU.is_gt, fill=0.0,
                                        base=0, pattern=[[-1, P]], channel_multiplier=1)
                nc.gpsimd.iota(INFO[:, :, 0].bitcast(I32), pattern=[[1, C]], base=0,
                               channel_multiplier=C).then_inc(s_id, 1)

            @block.tensor
            def _(pe):
                pe.wait_ge(s_id, 1)
                pe.wait_ge(s_w, 160)
                nc.tensor.transpose(PT[0][:, 0:D], W0R, ident[:, :]).then_inc(s_wT, 1)
                for n in range(2):
                    pe.wait_ge(s_diag, n + 1)
                    nc.tensor.matmul(PZ[n][0:P, 0, 0:P], ones[0:P, 0:P], DG[:, :],
                                     start=True, stop=True).then_inc(s_bc, 1)

            @block.vector
            def _(dve):
                ch = Chain(dve, "setup_chain")
                ch.add(nc.vector.memset(R[:, 0, :], 0.0))
                ch.add(nc.vector.memset(SD[:, :, :], 0.0))
                ch.add(nc.vector.memset(DH[:, :], NOWHERE))
                ch.wait()
                nc.vector.memset(fill[:, :, 0].bitcast(I32), NOWHERE).then_inc(s_halo, 1)
                nc.vector.memset(fill[:, :, 1], 1.0).then_inc(s_fill, 1)
                dve.wait_ge(s_w, 160)
                dve.wait_ge(s_wT, 1)
                ch.link(nc.vector.tensor_copy(W0[:, :], PT[0][:, 0:D]))
                ch.link(nc.vector.tensor_reduce(rowm, WR, AX.X, ALU.add))
                ch.link(nc.vector.tensor_scalar(rowm, rowm, 1.0 / D, None, ALU.mult))
                ch.link(nc.vector.tensor_tensor(WC[:, :, :], WR, rowm.unsqueeze(2).broadcast_to([D, L, D]),
                                                ALU.subtract))
                at = attb[:, :].rearrange("p (l f) -> p l f", l=L)
                for n, (w, o) in enumerate(((WR, SD[:, :, 0]), (WR, SD[:, :, 1]), (WER, VE[:, :]))):
                    dve.wait_ge(s_att, 16 * (n + 1))
                    nc.vector.tensor_tensor(PR, w, at, ALU.mult).then_inc(s_attf, 1)
                    dve.wait_ge(s_attf, n + 1)
                    ch.link(nc.vector.tensor_reduce(o, PR, AX.X, ALU.add))
                ch.link(nc.vector.tensor_reduce(bm[:, 0:L], brow[:, 0:L, :], AX.X, ALU.add))
                ch.link(nc.vector.tensor_scalar(bm[:, 0:L], bm[:, 0:L], 1.0 / D, None, ALU.mult))
                ch.link(nc.vector.tensor_tensor(brow[:, 0:L, :], brow[:, 0:L, :],
                                                bm[:, 0:L].unsqueeze(2).broadcast_to([1, L, D]), ALU.subtract))
                ch.link(nc.vector.tensor_copy(bpart[:, 0, :, :], brow))
                ch.link(nc.vector.tensor_tensor(blo, brow, bpart[:, 0, :, :], ALU.subtract))
                ch.link(nc.vector.tensor_copy(bpart[:, 1, :, :], blo))
                ch.link(nc.vector.tensor_tensor(blo, blo, bpart[:, 1, :, :], ALU.subtract))
                nc.vector.tensor_copy(bpart[:, 2, :, :], blo).then_inc(s_bs, 1)
                dve.wait_ge(s_meta, 64)
                dve.wait_ge(s_id, 1)
                ch.link(nc.vector.tensor_copy(DF, DH))
                cur = DF[:, 1:C + 1]
                ch.add(nc.vector.tensor_tensor(keep[:, :], cur, DF[:, 0:C], ALU.is_equal))
                ch.add(nc.vector.tensor_tensor(rep[:, :], cur, DF[:, 2:C + 2], ALU.not_equal))
                ch.add(nc.vector.tensor_tensor(knext[:, :], cur, DF[:, 2:C + 2], ALU.is_equal))
                ch.add(nc.vector.tensor_scalar(first[:, :], cur, DF[:, 1:2], None, ALU.is_equal))
                for c0, c1 in ((0, HALF * Q), (HALF * Q, C)):
                    ch.add(nc.vector.tensor_scalar(cont[:, c0:c1], cur[:, c0:c1], DF[:, c0:c0 + 1] if c0 else
                                                   DF[:, 1:2], None, ALU.is_equal))
                ch.add(nc.vector.tensor_scalar(last[:, :], cur, DF[:, C:C + 1], None, ALU.is_equal))
                ch.wait()
                ch.add(nc.vector.tensor_scalar(pen[:, :], keep[:, :], -1.0, BIG, ALU.add, ALU.mult))
                ch.add(nc.vector.tensor_scalar(penf[:, :], first[:, :], -1.0, BIG, ALU.add, ALU.mult))
                ch.link(nc.vector.tensor_scalar(tmp[:, :], cur, -float(NOWHERE), None, ALU.add))
                ch.link(nc.vector.tensor_tensor(tmp[:, :], tmp[:, :], rep[:, :], ALU.mult))
                ch.link(nc.vector.tensor_scalar(tmp[:, :], tmp[:, :], float(NOWHERE), None, ALU.add))
                ch.link(nc.vector.tensor_copy(repI[:, :], tmp[:, :]))
                nc.vector.tensor_scalar(DG[:, :], ident[0:P, 0:P], DF[:, 1:2], None, ALU.mult).then_inc(s_diag, 1)
                dve.wait_ge(s_bc, 1)
                ch.link(nc.vector.scalar_tensor_tensor(MF[:, :], PZ[0][0:P, 0, 0:P], DF[:, C:C + 1], MF[:, :],
                                                       ALU.is_equal, ALU.mult))
                nc.vector.tensor_scalar(DG[:, :], ident[0:P, 0:P], DF[:, C:C + 1], None, ALU.mult).then_inc(s_diag, 1)
                dve.wait_ge(s_bc, 2)
                ch.link(nc.vector.scalar_tensor_tensor(MB[:, :], PZ[1][0:P, 0, 0:P], DF[:, 1:2], MB[:, :],
                                                       ALU.is_equal, ALU.mult))
                ch.link(nc.vector.tensor_scalar(PM[:, :], MB[:, :], -1.0, BIG, ALU.add, ALU.mult))

        class Segments:

            def __init__(self, dve):
                self.dve, self.ch = dve, Chain(dve, "segment_chain")
                self.asked, self.carried = signal("carry_asked", "carried")
                self.n = 0

            def carry(self, ins):
                self.n += 1
                ins.then_inc(self.asked.s, 1)
                self.dve.wait_ge(*self.carried.at(self.n))

            def end(self):
                self.ch.end()
                self.asked.base += self.n
                self.carried.base += self.n

            def total(self, o, v):
                self.carry(nc.vector.tensor_tensor_scan(o, keep[:, :], v, 0.0, ALU.mult, ALU.add))
                self.ch.link(nc.vector.tensor_copy(car1[:, 0:1], PZ[3][0:P, 0, 0:1]))
                self.ch.link(nc.vector.scalar_tensor_tensor(o, first[:, :], car1[:, 0:1], o, ALU.mult, ALU.add))

            def spread(self, o, v, t):
                self.ch.link(nc.vector.tensor_tensor(t, v, rep[:, :], ALU.mult))
                self.carry(nc.vector.tensor_tensor_scan(o[:, ::-1], knext[:, ::-1], t[:, ::-1], 0.0,
                                                        ALU.mult, ALU.add))
                self.ch.link(nc.vector.tensor_copy(car1[:, 0:1], PZ[3][0:P, 0, 0:1]))
                self.ch.link(nc.vector.scalar_tensor_tensor(o, last[:, :], car1[:, 0:1], o, ALU.mult, ALU.add))

            def maximum(self, o, v):
                ch = self.ch
                ch.link(nc.vector.tensor_tensor_scan(o, pen[:, :], v, -BIG, ALU.add, ALU.max))
                self.carry(nc.vector.tensor_scalar(DG[:, :], ident[0:P, 0:P], o[:, C - 1:C], None, ALU.mult))
                ch.link(nc.vector.tensor_tensor(DG[:, :], PZ[3][0:P, 0, 0:P], PM[:, :], ALU.add))
                ch.link(nc.vector.tensor_reduce(car1[:, 0:1], DG[:, :], AX.X, ALU.max))
                ch.link(nc.vector.tensor_scalar(tmp[:, :], penf[:, :], car1[:, 0:1], None, ALU.add))
                ch.link(nc.vector.tensor_tensor(o, o, tmp[:, :], ALU.max))

        def carries(pe, seg, steps):
            for n, (kind, o) in enumerate(steps):
                pe.wait_ge(*seg.asked.at(n + 1))
                if kind == "total":
                    ins = nc.tensor.matmul(PZ[3][0:P, 0, 0:1], MF[:, :], o[:, C - 1:C], start=True, stop=True)
                elif kind == "spread":
                    ins = nc.tensor.matmul(PZ[3][0:P, 0, 0:1], MB[:, :], o[:, 0:1], start=True, stop=True)
                else:
                    ins = nc.tensor.matmul(PZ[3][0:P, 0, 0:P], ones[0:P, 0:P], DG[:, :], start=True, stop=True)
                ins.then_inc(seg.carried.s, 1)

        s_deg = sem("info_ready")
        s_degm = sem("degree_ready")
        s_degr = sem("degree_root_ready")
        s_eaT = sem("edge_attr_transposed")
        s_eac = sem("edge_attr_transposed_copied")
        s_aep = sem("edge_term_ready")
        s_aes = sem("edge_term_stored")
        EG = C // Q
        XSRC_EARLY = C // 2
        with nc.Block() as block:
            segbox = []

            @block.gpsimd
            def _(pool):
                gather_x(pool, S, srcI, 0, XSRC_EARLY, s_xsrc)

            @block.vector
            def _(dve):
                seg = Segments(dve)
                segbox.append(seg)
                ch = seg.ch
                ch.link(nc.vector.memset(lg[:, :], 1.0))
                seg.total(run[:, :], lg[:, :])
                nc.vector.tensor_scalar(lg[:, :], run[:, :], 1.0, None, ALU.max).then_inc(s_degm, 1)
                dve.wait_ge(s_degr, 1)
                ch.link(nc.vector.reciprocal(mx[:, :], ls[:, :]))
                nc.vector.tensor_copy(INFO[:, :, 1], mx[:, :]).then_inc(s_deg, 1)
                seg.spread(isq[:, :], mx[:, :], tmp[:, :])
                ch.link(nc.vector.reciprocal(mx[:, :], lg[:, :]))
                for g in range(EG):
                    dve.wait_ge(s_aep, g + 1)
                    nc.vector.tensor_copy(AE[:, g * Q:(g + 1) * Q, :],
                                          PZ[g % 2][0:P, 0, 0:Q * L].rearrange("p (a l) -> p a l", a=Q)).then_inc(s_aes, 1)
                dve.wait_ge(s_aes, EG)
                for l in range(L):
                    ch.link(nc.vector.tensor_copy(ls[:, :], AE[:, :, l]))
                    seg.total(lg[:, :], ls[:, :])
                    ch.link(nc.vector.tensor_tensor(AL[:, :, l], lg[:, :], mx[:, :], ALU.mult))

            @block.tensor
            def _(pe):
                seg = segbox[0]
                carries(pe, seg, [("total", run[:, :]), ("spread", isq[:, :])])
                pe.wait_ge(s_ea, 32)

                def transpose(g):
                    if g >= 2:
                        pe.wait_ge(s_eac, g - 1)
                    transposes(PT[g % 2], [R[:, 1 + g * Q + a, :] for a in range(Q)]).then_inc(s_eaT, 1)

                transpose(0)
                for g in range(EG):
                    if g + 1 < EG:
                        transpose(g + 1)
                    pe.wait_ge(s_eac, g + 1)
                    if g >= 2:
                        pe.wait_ge(s_aes, g - 1)
                    for a in range(Q):
                        ins = nc.tensor.matmul(PZ[g % 2][0:P, 0, a * L:(a + 1) * L],
                                               XT[:, g % 2, a * P:(a + 1) * P], VE[:, :], start=True, stop=True)
                    ins.then_inc(s_aep, 1)
                for l in range(L):
                    pe.wait_ge(*seg.asked.at(3 + l))
                    nc.tensor.matmul(PZ[3][0:P, 0, 0:1], MF[:, :], lg[:, C - 1:C], start=True,
                                     stop=True).then_inc(seg.carried.s, 1)

            @block.scalar
            def _(act):
                act.wait_ge(s_degm, 1)
                nc.scalar.activation(ls[:, :], lg[:, :], ACT.Sqrt).then_inc(s_degr, 1)
                for g in range(EG):
                    act.wait_ge(s_eaT, g + 1)
                    if g >= 2:
                        act.wait_ge(s_aep, g - 1)
                    nc.scalar.activation(XT[:, g % 2, :], PT[g % 2][:, 0:Q * P], ACT.Copy).then_inc(s_eac, 1)

        segbox[0].end()

        def dense(first_round, rounds, moves, move, arrive):
            loaded = signal("x_loaded_0", "x_loaded_1")
            stored = signal("out_stored_0", "out_stored_1")
            (y_ready, y_part, scales_ready, beta_added, t_done, xt_ready, z_done, slope_ready, sq_ready,
             var_ready, rt_ready, out_ready, summed, inverted, counted, leaked, joined, multiplied) = signal(
                "rows_ready", "rows_ready_scalar", "scales_ready", "beta_added", "transposed", "xt_ready",
                "product_done", "slope_ready", "squares_ready", "variance_ready", "root_ready", "out_ready",
                "last_squares_summed", "root_inverted", "statistics_done", "leaky_done", "residual_added",
                "gamma_multiplied")
            STEPS = 2 + L - 1
            K = STEPS * DS
            ITEMS = K + DS
            LN = 2 * DS

            def slots(eng, ahead, behind, slot):
                def turn(i, b):
                    first, final = (isinstance(i, int) and i == 0), (isinstance(i, int) and i == rounds - 1)

                    for n in range(-ahead if first else 0, ITEMS + (behind if final else 0)):
                        def item(offset):
                            m = n + offset
                            if m < 0:
                                return None if first else (i - 1, 1 - b, m + ITEMS)
                            if m >= ITEMS:
                                return None if final or m - ITEMS >= ITEMS else (i + 1, 1 - b, m - ITEMS)
                            return i, b, m
                        slot(item)

                turn(0, 0)
                if rounds > 3:
                    with eng.Fori(0, (rounds - 2) // 2) as ii:
                        turn(ii * 2 + 1, 1)
                        turn(ii * 2 + 2, 0)
                    rest = (rounds - 2) // 2 * 2 + 1
                else:
                    rest = 1
                for i in range(rest, rounds):
                    turn(i, i % 2)

            with nc.Block() as block:
                @block.gpsimd
                def _(pool):
                    parts = rounds * DS
                    for n in range(parts):
                        i, s = divmod(n, DS)
                        move(pool, moves * n // parts, moves * (n + 1) // parts)
                        pool.wait_ge(*t_done.at(i * K + DS + s + 1))
                        xs = X[:, i % 2, s * Q:(s + 1) * Q, :]
                        nc.gpsimd.tensor_tensor(xs, xs, B3[:, :].unsqueeze(1).broadcast_to([P, Q, D]),
                                                ALU.add).then_inc(beta_added.s, 1)
                    for done, value in arrive:
                        pool.wait_ge(done, value)

                @block.sync
                def _(sp):
                    for i in range(rounds + 2):
                        if i >= 2:
                            sp.wait_ge(*out_ready.at((i - 1) * DS))
                            dma2(sp, out_v[first_round + i - 2], X[:, i % 2, :, :], stored[i % 2].s)
                            sp.wait_ge(*stored[i % 2].at(32 * (i // 2)))
                        if i < rounds:
                            dma2(sp, X[:, i % 2, :, :], x_v[first_round + i], loaded[i % 2].s)

                @block.tensor
                def _(pe):
                    def product(i, b, n):
                        if n >= K:
                            return
                        k, s = divmod(n, DS)
                        pe.wait_ge(*xt_ready.at(i * K + (n + 1)))
                        w, bias = (W0[:, :], L) if k == 0 else (WC[:, k - 1, :], k - 1)
                        products(DPZ[s], XT[:, n % 4, :], w, bias).then_inc(z_done.s, 1)

                    def transpose(i, b, n):
                        if n >= K:
                            return
                        s = n % DS
                        pe.wait_ge(*y_ready.at(i * K + (n + 1)))
                        if n < LN:
                            pe.wait_ge(*y_part.at(i * LN + (n + 1)))
                        transposes(DPT[n % 3], [Y[:, s, a, :] for a in range(Q)]).then_inc(t_done.s, 1)

                    def slot(item):
                        for offset, op in ((-2, product), (0, transpose)):
                            if item(offset):
                                op(*item(offset))

                    slots(pe, 0, 2, slot)

                @block.scalar
                def _(act):
                    def root(i, b, n):
                        k, s = divmod(n, DS)
                        if k == STEPS:
                            act.wait_ge(*summed.at(i * DS + (s + 1)))
                        else:
                            act.wait_ge(*var_ready.at(i * K + (n + 1)))
                        roots(mv[:, s, :, 1] if k < 2 else ss[:, s, :], s).then_inc(rt_ready.s, 1)

                    def copy_transposed(i, b, n):
                        if n >= K:
                            return
                        k, s = divmod(n, DS)
                        act.wait_ge(*t_done.at(i * K + (n + 1)))
                        if k < 2:
                            ins = nc.scalar.activation(XT[:, n % 4, :], DPT[n % 3][:, 0:Q * P], ACT.Relu)
                        else:
                            ins = nc.scalar.activation(XT[:, n % 4, :], DPT[n % 3][:, 0:Q * P], ACT.Identity,
                                                       bias=BC[:, k - 2:k - 1], scale=GC[:, k - 2:k - 1])
                        ins.then_inc(xt_ready.s, 1)

                    def square(i, b, n):
                        if n >= K:
                            return
                        k, s = divmod(n, DS)
                        act.wait_ge(*z_done.at(i * K + (n + 1)))
                        if k == 0:
                            nc.scalar.mul(Y[:, s, :, :], DPZ[s][0:P, :, :], 0.01).then_inc(slope_ready.s, 1)
                        elif k == STEPS - 1:
                            for a in range(Q):
                                ins = nc.scalar.activation(Y[:, s, a, :], DPZ[s][0:P, a, :], ACT.Square,
                                                           scale=D ** -0.5, accum_out=ss[:, s, a:a + 1])
                            ins.then_inc(summed.s, 1)
                        else:
                            nc.scalar.activation(Y[:, s, :, :], DPZ[s][0:P, :, :], ACT.Square,
                                                 scale=D ** -0.5).then_inc(sq_ready.s, 1)

                    def normalise_part(i, b, n):
                        if n >= LN:
                            return
                        k, s = divmod(n, DS)
                        act.wait_ge(*scales_ready.at(i * LN + (n + 1)))
                        for a in range(ACT_TILES[k]):
                            ins = nc.scalar.activation(Y[:, s, a, :], X[:, b, s * Q + a, :], ACT.Identity,
                                                       bias=nm[:, s, a:a + 1], scale=rr[:, s, a:a + 1])
                        ins.then_inc(y_part.s, 1)

                    def slot(item):
                        for offset, op in ((-3, square), (1, root), (-1, copy_transposed), (0, normalise_part)):
                            if item(offset):
                                op(*item(offset))

                    slots(act, 1, 3, slot)

                @block.vector
                def _(dve):
                    def rows(b, s):
                        return X[:, b, s * Q:(s + 1) * Q, :]

                    def statistics(b, n):
                        s = n % DS
                        take_wait(0)
                        for a in range(Q):
                            ins = nc.vector.bn_stats(st[:, n % 2, a, :], rows(b, s)[:, a, :])
                        ins.then_inc(counted.s, 1)

                    def begin(i, b, n):
                        k, s = divmod(n, DS)
                        if k == 0:
                            if s == 0:
                                dve.wait_ge(*loaded[b].at((i - b) * 16 + 32))
                            statistics(b, n)
                        elif k == 1:
                            dve.wait_ge(*slope_ready.at(i * DS + (s + 1)))
                            nc.vector.tensor_tensor(Y[:, s, :, :], Y[:, s, :, :], DPZ[s][0:P, :, :],
                                                    ALU.max).then_inc(leaked.s, 1)
                        elif k < STEPS:
                            dve.wait_ge(*sq_ready.at(i * ((L - 1) * DS) + (n - LN + 1)))
                            nc.vector.tensor_reduce(ss[:, s, :], Y[:, s, :, :], AX.X,
                                                    ALU.add).then_inc(var_ready.s, 1)

                    def join(i, b, n):
                        k, s = divmod(n, DS)
                        if k == 1:
                            dve.wait_ge(*leaked.at(i * DS + (s + 1)))
                            nc.vector.tensor_tensor(rows(b, s), rows(b, s), Y[:, s, :, :],
                                                    ALU.add).then_inc(joined.s, 1)

                    def measure(i, b, n):
                        k, s = divmod(n, DS)
                        if k == 1:
                            dve.wait_ge(*joined.at(i * DS + (s + 1)))
                            statistics(b, n)

                    def aggregate(i, b, n):
                        if n < LN:
                            dve.wait_ge(*counted.at(i * LN + (n + 1)))
                            take_wait(1)
                            for a in range(Q):
                                ins = nc.vector.bn_aggr(mv[:, n % DS, a, :], st[:, n % 2, a, :])
                            ins.then_inc(var_ready.s, 1)

                    def invert(i, b, n):
                        s = n % DS
                        dve.wait_ge(*rt_ready.at(i * ITEMS + (n + 1)))
                        nc.vector.reciprocal(rr[:, s, :], rt[:, s, :]).then_inc(inverted.s, 1)

                    def scale(i, b, n):
                        s = n % DS
                        if n < LN:
                            dve.wait_ge(*inverted.at(i * ITEMS + (n + 1)))
                            nc.vector.scalar_tensor_tensor(nm[:, s, :], mv[:, s, :, 0], -1.0, rr[:, s, :], ALU.mult,
                                                           ALU.mult).then_inc(scales_ready.s, 1)

                    def normalise(i, b, n):
                        k, s = divmod(n, DS)
                        if k < 2:
                            dve.wait_ge(*scales_ready.at(i * LN + (n + 1)))
                            for a in range(ACT_TILES[k], Q):
                                ins = nc.vector.tensor_scalar(
                                    Y[:, s, a, :], rows(b, s)[:, a, :], rr[:, s, a:a + 1], nm[:, s, a:a + 1],
                                    ALU.mult, ALU.add)
                            ins.then_inc(y_ready.s, 1)
                            return
                        dve.wait_ge(*inverted.at(i * ITEMS + (n + 1)))
                        if k < STEPS:
                            nc.vector.tensor_tensor(Y[:, s, :, :], DPZ[s][0:P, :, :],
                                                    wide(rr[:, s, :]), ALU.mult).then_inc(y_ready.s, 1)
                            return
                        for a in range(Q):
                            ins = nc.vector.scalar_tensor_tensor(
                                Y[:, s, a, :], DPZ[s][0:P, a, :], rr[:, s, a:a + 1], G3[:, :], ALU.mult, ALU.mult)
                        ins.then_inc(multiplied.s, 1)

                    def finish(i, b, n):
                        k, s = divmod(n, DS)
                        if k == STEPS:
                            dve.wait_ge(*multiplied.at(i * DS + (s + 1)))
                            dve.wait_ge(*beta_added.at(i * DS + (s + 1)))
                            nc.vector.tensor_tensor(rows(b, s), rows(b, s), Y[:, s, :, :],
                                                    ALU.add).then_inc(out_ready.s, 1)

                    def slot(item):
                        for offset, op in ((0, normalise), (-1, finish), (1, aggregate), (2, begin), (1, invert), (2, join), (1, scale), (2, measure)):
                            if item(offset):
                                op(*item(offset))

                    slots(dve, 2, 1, slot)

            for sig, each in ((y_ready, K), (t_done, K), (xt_ready, K), (z_done, K), (slope_ready, DS),
                              (y_part, LN), (scales_ready, LN), (beta_added, DS), (summed, DS),
                              (sq_ready, (L - 1) * DS), (var_ready, K), (rt_ready, ITEMS), (out_ready, DS),
                              (inverted, ITEMS), (counted, LN), (leaked, DS), (joined, DS), (multiplied, DS)):
                sig.base += each * rounds
            for b in range(2):
                loaded[b].base += 32 * ((rounds - b + 1) // 2)
                stored[b].base += 32 * ((rounds - b + 1) // 2)

        G = C // Q

        BOTH = list(range(Q)) + list(range(HALF * Q, HALF * Q + Q))

        def staggered(eng, items, ops, unrolled=False, then=None):
            def slot(t, u):
                for offset, op in (then if then and t >= HALF else ops):
                    if 0 <= t - offset < items:
                        op(t - offset, (u - offset) % NS)

            end = items + max(offset for offset, _ in ops)
            if unrolled:
                for t in range(end):
                    slot(t, t % NS)
                return
            head = -(-max(offset for offset, _ in ops) // NS) or 1
            for t in range(head * NS):
                slot(t, t % NS)
            parts = [(head, HALF // NS, ops), (HALF // NS, items // NS, then)] if then else [
                (head, items // NS, ops)]
            for first_turn, turns, part in parts:
                with eng.Fori(first_turn, turns) as i:
                    for u in range(NS):
                        for offset, op in part:
                            op(i * NS + (u - offset), (u - offset) % NS)
            for t in range(items // NS * NS, end):
                slot(t, t % NS)

        def group(buf, n, shift=0):
            if isinstance(n, int):
                return buf[:, n * Q + shift:n * Q + shift + Q]
            return buf[:, bass.ds(n * Q + shift, Q)]

        def column(buf, n, a, shift=0):
            if isinstance(n, int):
                return buf[:, n * Q + a + shift]
            return buf[:, bass.ds(n * Q + (a + shift), 1)].rearrange("p a f -> p (a f)")

        def scalar_of(buf, n, a):
            if isinstance(n, int):
                return buf[:, n * Q + a:n * Q + a + 1]
            return buf[:, bass.ds(n * Q + a, 1)]

        def run_on(n, a):
            return nc.vector.scalar_tensor_tensor(column(R, n, a, 1), column(R, n, a, 0), scalar_of(keep, n, a),
                                                  column(R, n, a, 1), ALU.mult, ALU.add)

        def add_carried(buf, n, a, shift=0):
            return nc.vector.scalar_tensor_tensor(column(buf, n, a, shift), CAR[:, :], scalar_of(first, n, a),
                                                  column(buf, n, a, shift), ALU.mult, ALU.add)

        class Norm:

            def __init__(self, name, frm, to, on_scalar, which):
                self.st, self.t = st[:, 2 * which:2 * which + 2], 4 * which
                self.frm, self.to, self.k = frm, to, on_scalar
                self.mv, self.rt = sb(name + "_mv", [P, NS, Q, 2]), sb(name + "_rt", [P, NS, Q])
                self.rr, self.nm = sb(name + "_rr", [P, NS, Q]), sb(name + "_nm", [P, NS, Q])
                (self.counted, self.aggregated, self.rooted, self.inverted, self.scaled, self.by_scalar,
                 self.by_vector) = (
                    sem(name + n) for n in ("_counted", "_aggregated", "_rooted", "_inverted", "_scaled", "_by_scalar",
                                            "_by_vector"))

            def statistics(self, n, r):
                v = self.frm(n, r)
                take_wait(self.t + r % 2 * 2)
                for a in range(Q):
                    ins = nc.vector.bn_stats(self.st[:, r % 2, a, :], v[:, a, :])
                ins.then_inc(self.counted, 1)

            def aggregate(self, n, r):
                self.dve.wait_ge(self.counted, n + 1)
                take_wait(self.t + r % 2 * 2 + 1)
                for a in range(Q):
                    ins = nc.vector.bn_aggr(self.mv[:, r, a, :], self.st[:, r % 2, a, :])
                ins.then_inc(self.aggregated, 1)

            def root(self, act, n, r):
                act.wait_ge(self.aggregated, n + 1)
                nc.scalar.activation(self.rt[:, r, :], self.mv[:, r, :, 1], ACT.Sqrt,
                                     bias=epsc[:, 0:1]).then_inc(self.rooted, 1)

            def invert(self, n, r):
                self.dve.wait_ge(self.rooted, n + 1)
                nc.vector.reciprocal(self.rr[:, r, :], self.rt[:, r, :]).then_inc(self.inverted, 1)

            def scale(self, n, r):
                self.dve.wait_ge(self.inverted, n + 1)
                nc.vector.scalar_tensor_tensor(self.nm[:, r, :], self.mv[:, r, :, 0], -1.0, self.rr[:, r, :],
                                               ALU.mult, ALU.mult).then_inc(self.scaled, 1)

            def normal_scalar(self, act, n, r):
                act.wait_ge(self.scaled, n + 1)
                v, o = self.frm(n, r), self.to(n, r)
                for a in range(self.k):
                    ins = nc.scalar.activation(o[:, a, :], v[:, a, :], ACT.Identity,
                                               bias=self.nm[:, r, a:a + 1], scale=self.rr[:, r, a:a + 1])
                ins.then_inc(self.by_scalar, 1)

            def normal_vector(self, n, r):
                if self.k < Q:
                    self.dve.wait_ge(self.scaled, n + 1)
                    v, o = self.frm(n, r), self.to(n, r)
                    for a in range(self.k, Q):
                        ins = nc.vector.tensor_scalar(o[:, a, :], v[:, a, :], self.rr[:, r, a:a + 1],
                                                      self.nm[:, r, a:a + 1], ALU.mult, ALU.add)
                    ins.then_inc(self.by_vector, 1)

            def wait(self, eng, n):
                eng.wait_ge(self.by_scalar, n + 1)
                if self.k < Q:
                    eng.wait_ge(self.by_vector, n + 1)

        def carry_in(parts):
            brought, ended, copied = signal("carry_product", "run_ended", "carry_copied")
            middle = HALF * Q
            with nc.Block() as block:
                @block.tensor
                def _(pe):
                    if parts == 2:
                        pe.wait_ge(*ended.at(1))
                    nc.tensor.matmul(PZ[0][0:P, 0, :], MF[:, :], END[:, :] if parts == 2 else R[:, C, :],
                                     start=True, stop=True).then_inc(brought.s, 1)

                @block.scalar
                def _(act):
                    act.wait_ge(*brought.at(1))
                    nc.scalar.activation(CAR[:, :], PZ[0][0:P, 0, :], ACT.Copy).then_inc(copied.s, 1)

                if parts == 2:
                    @block.vector
                    def _(dve):
                        nc.vector.scalar_tensor_tensor(END[:, :], R[:, middle, :], cont[:, C - 1:C], R[:, C, :],
                                                       ALU.mult, ALU.add).then_inc(ended.s, 1)
                        dve.wait_ge(*copied.at(1))
                        nc.vector.scalar_tensor_tensor(CAR2[:, :], CAR[:, :], cont[:, middle - 1:middle],
                                                       R[:, middle, :], ALU.mult, ALU.add)
            brought.base += 1
            copied.base += 1
            ended.base += parts - 1

        s_iscat = sem("info_scattered")
        s_igat = sem("info_gathered")

        def first_moves(pool, a, b):
            for m in range(a + XSRC_EARLY, b + XSRC_EARLY):
                step, c = divmod(m, C)
                if step == 0:
                    gather_x(pool, S, srcI, c, c + 1, s_xsrc)
                elif step == 1:
                    scatter(pool, info_t, repI[:, c:c + 1], N, INFO[:, c, :], s_iscat)
                elif step == 2:
                    gather_x(pool, T, dstI, c, c + 1, s_xdst)
                else:
                    if c == 0:
                        pool.wait_ge(s_iscat, 16 * C)
                    gather(pool, INFG[:, c, :], srcI[:, c:c + 1], info_t, N, s_igat)

        dense(0, SHARES[0], 4 * C - XSRC_EARLY, first_moves,
              [(s_xsrc, 16 * C), (s_xdst, 16 * C), (s_igat, 16 * C)])

        s_alpha = sem("conv_alpha_ready")
        t_done, xt_ready, z_done, m_ready, biased, slope_ready, leaky_ready, run_done, x1_ready = (
            sem("convS_" + n) for n in ("transposed", "xt_ready", "product_done", "message_ready",
                                        "bias_added", "slope_ready", "leaky_ready", "run_done", "x1_ready"))
        ln1 = Norm("convS_ln1", lambda n, r: group(S, n), lambda n, r: Y[:, r, :, :], 2, 0)
        ln2 = Norm("convS_ln2", lambda n, r: group(S, n), lambda n, r: group(S, n), 2, 1)

        def rows_free(eng, n):
            if not isinstance(n, int) or n >= NS:
                eng.wait_ge(x1_ready, n - (NS - 1))

        with nc.Block() as block:
            @block.tensor
            def _(pe):
                def transpose(n, r):
                    ln1.wait(pe, n)
                    transposes(PT[r], [Y[:, r, a, :] for a in range(Q)]).then_inc(t_done, 1)

                def product(n, r):
                    pe.wait_ge(xt_ready, n + 1)
                    products(PZ[r], XT[:, r, :], W0[:, :], None).then_inc(z_done, 1)

                def add_bias(n, r):
                    pe.wait_ge(m_ready, n + 1)
                    nc.tensor.matmul(PZ[r][0:P, :, :], ones3[:, 0:P], BR[:, L:L + 1, :].broadcast_to([3, Q, D]),
                                     start=False, stop=True, skip_group_check=True).then_inc(biased, 1)

                staggered(pe, G, [(3, product), (3, add_bias), (2, transpose)])

            @block.scalar
            def _(act):
                act.wait_ge(s_alpha, 1)

                def copy_transposed(n, r):
                    act.wait_ge(t_done, n + 1)
                    nc.scalar.activation(XT[:, r, :], PT[r][:, 0:Q * P], ACT.Relu).then_inc(xt_ready, 1)

                def message(n, r):
                    act.wait_ge(z_done, n + 1)
                    for a in range(Q):
                        ins = nc.scalar.activation(column(R, n, a, 1), PZ[r][0:P, a, :], ACT.Copy,
                                                   scale=scalar_of(alpha, n, a))
                    ins.then_inc(m_ready, 1)

                def slope(n, r):
                    act.wait_ge(biased, n + 1)
                    nc.scalar.mul(Y[:, r, :, :], PZ[r][0:P, :, :], 0.01).then_inc(slope_ready, 1)

                def normalise_part(n, r):
                    rows_free(act, n)
                    ln1.normal_scalar(act, n, r)

                staggered(act, G, [
                    (1, lambda n, r: ln1.root(act, n, r)), (7, lambda n, r: ln2.root(act, n, r)),
                    (3, copy_transposed), (2, normalise_part), (3, message),
                    (4, slope), (8, lambda n, r: ln2.normal_scalar(act, n, r))])

            @block.gpsimd
            def _(pool):
                def residual(n, r):
                    pool.wait_ge(leaky_ready, n + 1)
                    nc.gpsimd.tensor_tensor(group(S, n), group(S, n), Y[:, r, :, :], ALU.add).then_inc(x1_ready, 1)

                staggered(pool, G, [(0, residual)], unrolled=True)

            @block.vector
            def _(dve):
                c0 = Chain(dve, "convS_alpha_chain")
                c0.link(nc.vector.tensor_tensor(alpha[:, :], isq[:, :], wE[:, :], ALU.mult))
                nc.vector.tensor_tensor(alpha[:, :], alpha[:, :], INFG[:, :, 1], ALU.mult).then_inc(s_alpha, 1)
                ln1.dve = ln2.dve = dve

                def run(a):
                    def step(n, r):
                        if a == 0:
                            dve.wait_ge(m_ready, n + 1)
                        if a or not isinstance(n, int) or n:
                            dve.wait_ge(run_done, n * Q + a)
                        run_on(n, a).then_inc(run_done, 1)
                    return step

                def normalise_part(n, r):
                    rows_free(dve, n)
                    ln1.normal_vector(n, r)

                def leak(n, r):
                    dve.wait_ge(slope_ready, n + 1)
                    nc.vector.tensor_tensor(Y[:, r, :, :], Y[:, r, :, :], PZ[r][0:P, :, :],
                                            ALU.max).then_inc(leaky_ready, 1)

                def measure2(n, r):
                    dve.wait_ge(x1_ready, n + 1)
                    ln2.statistics(n, r)

                staggered(dve, G, [
                    (2, normalise_part), (8, ln2.normal_vector), (5, leak), (1, ln1.aggregate), (4, run(0)),
                    (7, ln2.aggregate), (0, ln1.statistics), (4, run(1)), (1, ln1.invert), (6, measure2),
                    (1, ln1.scale), (4, run(2)), (7, ln2.invert), (4, run(3)), (7, ln2.scale)])

        carry_in(parts=1)

        t_done2, xt_ready2, z_done2, carried2, summed2, leaky_ready2, x1_ready2 = (
            sem("convT_" + n) for n in ("transposed", "xt_ready", "product_done", "carried_added", "sum_ready",
                                        "leaky_ready", "x1_ready"))
        ln3 = Norm("convT_ln1", lambda n, r: group(T, n), lambda n, r: Y[:, r, :, :], Q, 0)
        ln4 = Norm("convT_ln2", lambda n, r: group(R, n, 1), lambda n, r: group(T, n), Q, 1)
        s_x1 = sem("x1_stored")
        s_rows = sem("rows_stored")
        STORE = 5
        STORES = G // STORE

        def rows_free2(eng, n):
            if not isinstance(n, int) or n >= NS:
                eng.wait_ge(x1_ready2, n - (NS - 1))

        with nc.Block() as block:
            @block.sync
            def _(sp):
                for i in range(STORES):
                    c0, c1 = i * STORE * Q, (i + 1) * STORE * Q
                    ln4.wait(sp, (i + 1) * STORE - 1)
                    dma2(sp, x1_v[:, c0:c1, :], R[:, c0 + 1:c1 + 1, :], s_x1)
                    dma2(sp, row_v[:, c0:c1, :], T[:, c0:c1, :], s_rows)
                sp.wait_ge(s_x1, 32 * STORES)
                sp.wait_ge(s_rows, 32 * STORES)

            @block.tensor
            def _(pe):
                def transpose(n, r):
                    ln3.wait(pe, n)
                    transposes(PT[r], [Y[:, r, a, :] for a in range(Q)]).then_inc(t_done2, 1)

                def product(n, r):
                    pe.wait_ge(xt_ready2, n + 1)
                    products(PZ[r], XT[:, r, :], W0[:, :], L).then_inc(z_done2, 1)

                staggered(pe, G, [(3, product), (2, transpose)])

            @block.scalar
            def _(act):
                def copy_transposed(n, r):
                    act.wait_ge(t_done2, n + 1)
                    nc.scalar.activation(XT[:, r, :], PT[r][:, 0:Q * P], ACT.Relu).then_inc(xt_ready2, 1)

                def normalise(n, r):
                    rows_free2(act, n)
                    ln3.normal_scalar(act, n, r)

                staggered(act, G, [
                    (1, lambda n, r: ln3.root(act, n, r)), (6, lambda n, r: ln4.root(act, n, r)),
                    (3, copy_transposed), (2, normalise), (7, lambda n, r: ln4.normal_scalar(act, n, r))])

            @block.gpsimd
            def _(pool):
                def residual(n, r):
                    pool.wait_ge(leaky_ready2, n + 1)
                    nc.gpsimd.tensor_tensor(group(R, n, 1), group(T, n), Y[:, r, :, :],
                                            ALU.add).then_inc(x1_ready2, 1)

                staggered(pool, G, [(0, residual)], unrolled=True)

            @block.vector
            def _(dve):
                ln3.dve = ln4.dve = dve

                def bring_in(n, r):
                    for a in range(Q):
                        ins = add_carried(R, n, a, 1)
                    ins.then_inc(carried2, 1)

                def add_product(n, r):
                    rg = group(R, n, 1)
                    dve.wait_ge(carried2, n + 1)
                    dve.wait_ge(z_done2, n + 1)
                    nc.vector.tensor_tensor(rg, rg, PZ[r][0:P, :, :], ALU.add).then_inc(summed2, 1)

                def leak(n, r):
                    dve.wait_ge(summed2, n + 1)
                    leaky(Y[:, r, :, :], group(R, n, 1), 0.01).then_inc(leaky_ready2, 1)

                def measure2(n, r):
                    dve.wait_ge(x1_ready2, n + 1)
                    ln4.statistics(n, r)

                staggered(dve, G, [
                    (4, add_product), (1, ln3.aggregate), (4, leak), (6, ln4.aggregate), (0, ln3.statistics),
                    (1, ln3.invert), (0, bring_in), (1, ln3.scale), (6, ln4.invert), (5, measure2),
                    (6, ln4.scale)])

        s_refresh = sem("s_refreshed")

        def refresh(pool, a, b):
            for c in range(a, b):
                gather(pool, S[:, c, :], INFG[:, c, 0:1].bitcast(I32), row_t, E, s_refresh)

        s_x1b = sem("x1_loaded")
        s_out = sem("out_scattered")

        def side_group(buf, n, r, shift=0):
            if isinstance(n, int):
                return group(buf, n // 2, shift)
            return buf[:, bass.ds(n * (Q // 2) + (shift - r % 2 * (Q // 2)), Q)]

        def attention(l):
            final = l == L - 1

            t_done, xt_ready, z_done, sq_ready, var_ready, rt_ready, copied, inverted, freed, scored = signal(
                "transposed", "xt_ready", "product_done", "squares_ready", "variance_ready", "root_ready",
                "message_copied", "root_inverted", "stream_freed", "scored")

            with nc.Block() as block:
                @block.tensor
                def _(pe):
                    def transpose(n, r):
                        buf, g = (S, T)[r % 2], n // 2
                        if n >= NS:
                            pe.wait_ge(*freed.at(n - NS + 1))
                        transposes(PT[r], [buf[:, g * Q + a, :] for a in range(Q)]).then_inc(t_done.s, 1)

                    def product(n, r):
                        pe.wait_ge(*xt_ready.at(n + 1))
                        if r % 2 == 0 and n >= NS:
                            pe.wait_ge(*copied.at(n - NS + 2))
                        products(PZ[r], XT[:, r, :], WC[:, l, :], l).then_inc(z_done.s, 1)

                    def scores(n, r):
                        for a in range(Q):
                            ins = nc.tensor.matmul(PT[r][0:P, a * D:a * D + SW], XT[:, r, a * P:(a + 1) * P],
                                                   SD[:, l, :], start=True, stop=True, skip_group_check=True)
                        ins.then_inc(scored.s, 1)

                    for t in range(0, 2 * G + 2, 2):
                        for op, n in ((product, t - 2), (product, t - 1), (transpose, t), (transpose, t + 1),
                                      (scores, t - 2), (scores, t - 1)):
                            if 0 <= n < 2 * G:
                                op(n, n % NS)

                @block.scalar
                def _(act):
                    def copy_transposed(n, r):
                        act.wait_ge(*t_done.at(n + 1))
                        if l == 0:
                            ins = nc.scalar.activation(XT[:, r, :], PT[r][:, 0:Q * P], ACT.Relu)
                        else:
                            ins = nc.scalar.activation(XT[:, r, :], PT[r][:, 0:Q * P], ACT.Identity,
                                                       bias=BC[:, l - 1:l], scale=GC[:, l - 1:l])
                        ins.then_inc(xt_ready.s, 1)

                    def message(n, r):
                        if r % 2:
                            return
                        act.wait_ge(*z_done.at(n + 1))
                        if not final:
                            nc.scalar.activation(Y[:, r, :, :], PZ[r][0:P, :, :], ACT.Square,
                                                 scale=D ** -0.5).then_inc(sq_ready.s, 2)
                        nc.scalar.activation(side_group(R, n, r, 1), PZ[r][0:P, :, :], ACT.Copy).then_inc(copied.s, 2)

                    def root(n, r):
                        if r % 2 or final:
                            return
                        act.wait_ge(*var_ready.at(n + 2))
                        roots(ss[:, r, :], r).then_inc(rt_ready.s, 2)

                    staggered(act, 2 * G, [(3, root), (0, copy_transposed), (2, message)], unrolled=False)

                @block.vector
                def _(dve):
                    def measure(n, r):
                        dve.wait_ge(*scored.at(n + 1))
                        sc = (SCS, SCT)[r % 2]
                        ins = nc.vector.tensor_copy(side_group(sc, n, r), tiles_of(PT[r])[0:P, :, 0:2])
                        if r % 2:
                            nc.vector.tensor_copy(side_group(T, n, r), PZ[r][0:P, :, :]).then_inc(freed.s, 1)
                        elif final:
                            ins.then_inc(freed.s, 1)
                        else:
                            dve.wait_ge(*sq_ready.at(n + 2))
                            nc.vector.tensor_reduce(ss[:, r, :], Y[:, r, :, :], AX.X,
                                                    ALU.add).then_inc(var_ready.s, 2)

                    def rescale(n, r):
                        if r % 2 or final:
                            return
                        dve.wait_ge(*rt_ready.at(n + 2))
                        nc.vector.reciprocal(rr[:, r, :], rt[:, r, :]).then_inc(inverted.s, 2)
                        dve.wait_ge(*inverted.at(n + 2))
                        nc.vector.tensor_tensor(side_group(S, n, r), PZ[r][0:P, :, :], wide(rr[:, r, :]),
                                                ALU.mult).then_inc(freed.s, 1)

                    staggered(dve, 2 * G, [(3, rescale), (2, measure)])

            for sig in (t_done, xt_ready, z_done, scored, freed):
                sig.base += 2 * G
            copied.base += 2 * G
            for sig in (sq_ready, var_ready, rt_ready, inverted):
                sig.base += 0 if final else 2 * G

            act_in, act_out = signal("exponents_ready", "exp_done")
            segbox = []
            with nc.Block() as block:
                @block.vector
                def _(dve):
                    seg = Segments(dve)
                    segbox.append(seg)
                    ch = seg.ch

                    def op(o, a, b, f):
                        ch.link(nc.vector.tensor_tensor(o[:, :], a, b, f))

                    seg.spread(run[:, :], SCT[:, :, 1], tmp[:, :])
                    op(lg, SCS[:, :, 0], run[:, :], ALU.add)
                    op(lg, lg[:, :], AE[:, :, l], ALU.add)
                    ch.link(nc.vector.scalar_tensor_tensor(lg[:, :], lg[:, :], 0.2, lg[:, :], ALU.mult, ALU.max))
                    op(ls, SCT[:, :, 0], SCT[:, :, 1], ALU.add)
                    op(ls, ls[:, :], AL[:, :, l], ALU.add)
                    ch.link(nc.vector.scalar_tensor_tensor(ls[:, :], ls[:, :], 0.2, ls[:, :], ALU.mult, ALU.max))
                    seg.maximum(mx[:, :], lg[:, :])
                    op(mx, mx[:, :], ls[:, :], ALU.max)
                    seg.spread(run[:, :], mx[:, :], tmp[:, :])
                    op(lg, lg[:, :], run[:, :], ALU.subtract)
                    op(ls, ls[:, :], run[:, :], ALU.subtract)
                    nc.vector.tensor_scalar(ls[:, :], ls[:, :], 0.0, None, ALU.min).then_inc(act_in.s, 1)
                    dve.wait_ge(*act_out.at(2))
                    seg.total(run[:, :], alpha[:, :])
                    op(run, run[:, :], aself[:, :], ALU.add)
                    ch.link(nc.vector.tensor_scalar(run[:, :], run[:, :], 1e-16, None, ALU.add))
                    seg.spread(mx[:, :], run[:, :], tmp[:, :])
                    ch.link(nc.vector.reciprocal(mx[:, :], mx[:, :]))
                    op(alpha, alpha[:, :], mx[:, :], ALU.mult)
                    op(aself, aself[:, :], mx[:, :], ALU.mult)

                @block.tensor
                def _(pe):
                    carries(pe, segbox[0], [("spread", run[:, :]), ("max", None), ("spread", run[:, :]),
                                            ("total", run[:, :]), ("spread", mx[:, :])])

                @block.scalar
                def _(act):
                    act.wait_ge(*act_in.at(1))
                    nc.scalar.activation(alpha[:, :], lg[:, :], ACT.Exp).then_inc(act_out.s, 1)
                    nc.scalar.activation(aself[:, :], ls[:, :], ACT.Exp).then_inc(act_out.s, 1)

                @block.sync
                def _(sp):
                    if final:
                        dma2(sp, S, x1_v, s_x1b)
                        sp.wait_ge(s_x1b, 32)

            segbox[0].end()
            act_in.base += 1
            act_out.base += 2

            weighted, run_done = signal("messages_weighted", "run_done")
            with nc.Block() as block:
                @block.scalar
                def _(act):
                    def weigh(n, r):
                        for a in BOTH if not isinstance(n, int) or n < HALF else range(Q):
                            ins = nc.scalar.activation(column(R, n, a, 1), column(R, n, a, 1), ACT.Copy,
                                                       scale=scalar_of(alpha, n, a))
                        ins.then_inc(weighted.s, 1)

                    staggered(act, HALF, [(0, weigh)])
                    weigh(G - 1, 0)

                @block.vector
                def _(dve):
                    def self_loop(n, a):
                        nc.vector.scalar_tensor_tensor(
                            column(T, n, a), column(T, n, a), scalar_of(aself, n, a), column(R, n, a, 1),
                            ALU.mult, ALU.add)

                    def step(n, a):
                        start = isinstance(n, int) and n == 0 and a == 0
                        if not start:
                            dve.wait_ge(*run_done.at(n * (2 * Q) + (2 * a - 1)))
                        run_on(n, a).then_inc(run_done.s, 1)
                        if not start:
                            run_on(n, a + HALF * Q).then_inc(run_done.s, 1)
                            self_loop(n, a - 1)
                            self_loop(n, a - 1 + HALF * Q)

                    def run(n, r):
                        dve.wait_ge(*weighted.at(n + 1))
                        for a in range(Q):
                            step(n, a)

                    staggered(dve, HALF, [(0, run)])
                    dve.wait_ge(*run_done.at(2 * HALF * Q - 1))
                    self_loop(HALF - 1, Q - 1)
                    dve.wait_ge(*weighted.at(HALF + 1))
                    for c in range(2 * HALF * Q, C):
                        dve.wait_ge(*run_done.at(c - 1))
                        run_on(0, c).then_inc(run_done.s, 1)
                        self_loop(0, c - 1)
                    dve.wait_ge(*run_done.at(C - 1))
                    self_loop(0, C - 1)

                if final:
                    @block.gpsimd
                    def _(pool):
                        def add_beta(n, r):
                            nc.gpsimd.tensor_tensor(group(S, n), group(S, n),
                                                    B3[:, :].unsqueeze(1).broadcast_to([P, Q, D]), ALU.add)
                        staggered(pool, G, [(0, add_beta)], unrolled=True)

            weighted.base += HALF + 1
            run_done.base += C - 1
            carry_in(parts=2)

            sum_ready, summed, rt_ready2, inverted2, scaled, t_ready = signal(
                "sum_ready", "sum_squares_summed", "root_ready", "root_inverted", "gamma_applied", "t_rows_final")
            with nc.Block() as block:
                @block.vector
                def _(dve):
                    def bring_in(carried):
                        def op(n, r):
                            for a in range(Q):
                                ins = nc.vector.scalar_tensor_tensor(
                                    column(T, n, a), carried[:, :], scalar_of(cont, n, a), column(T, n, a),
                                    ALU.mult, ALU.add)
                            ins.then_inc(sum_ready.s, 1)
                        return op

                    def rescale(n, r):
                        dve.wait_ge(*rt_ready2.at(n + 1))
                        nc.vector.reciprocal(rr[:, r, :], rt[:, r, :]).then_inc(inverted2.s, 1)
                        dve.wait_ge(*inverted2.at(n + 1))
                        tg = group(T, n)
                        if not final:
                            nc.vector.tensor_tensor(tg, tg, wide(rr[:, r, :]), ALU.mult).then_inc(t_ready.s, 1)
                            return
                        for a in range(Q):
                            ins = nc.vector.scalar_tensor_tensor(
                                column(T, n, a), column(T, n, a), rr[:, r, a:a + 1], G3[:, :], ALU.mult, ALU.mult)
                        ins.then_inc(scaled.s, 1)
                        dve.wait_ge(*scaled.at(n + 1))
                        nc.vector.tensor_tensor(tg, tg, group(S, n), ALU.add).then_inc(t_ready.s, 1)

                    staggered(dve, G, [(2, rescale), (0, bring_in(CAR))], then=[(2, rescale), (0, bring_in(CAR2))])

                @block.scalar
                def _(act):
                    def square(n, r):
                        act.wait_ge(*sum_ready.at(n + 1))
                        for a in range(Q):
                            ins = nc.scalar.activation(Y[:, r, a, :], column(T, n, a), ACT.Square,
                                                       scale=D ** -0.5, accum_out=ss[:, r, a:a + 1])
                        ins.then_inc(summed.s, 1)

                    def root(n, r):
                        act.wait_ge(*summed.at(n + 1))
                        roots(ss[:, r, :], r).then_inc(rt_ready2.s, 1)

                    staggered(act, G, [(1, root), (0, square)])

                if final:
                    @block.gpsimd
                    def _(pool):
                        for c in range(C):
                            pool.wait_ge(*t_ready.at(c // Q + 1))
                            scatter(pool, out, repI[:, c:c + 1], N, T[:, c, :], s_out)
                        pool.wait_ge(s_out, 16 * C)
                else:
                    @block.sync
                    def _(sp):
                        for i in range(STORES):
                            c0, c1 = i * STORE * Q, (i + 1) * STORE * Q
                            sp.wait_ge(*t_ready.at((i + 1) * STORE))
                            dma2(sp, row_v[:, c0:c1, :], T[:, c0:c1, :], s_rows)
                        sp.wait_ge(s_rows, 32 * STORES * (l + 2))

            for sig in (sum_ready, summed, rt_ready2, inverted2, t_ready):
                sig.base += G

        done = SHARES[0]
        for l in range(L):
            dense(done, SHARES[l + 1], C, refresh, [(s_refresh, 16 * C * (l + 1))])
            done += SHARES[l + 1]
            attention(l)
        assert done == ROUNDS


_INS = ["x", "src", "dst", "edge_attr_128", "edge_weight", "L0_gnn_W_weight", "L0_gnn_W_bias", "L1_gnn_W",
        "L1_gnn_We", "L1_gnn_att_src", "L1_gnn_att_dst", "L1_gnn_att_edge", "L1_gnn_bias",
        "L1_gnn_ln_gamma", "L1_gnn_ln_beta"]


def kernel(**inputs):
    import numpy as np
    import concourse.bacc as bacc
    from concourse.bass_utils import run_bass_kernel_spmd

    nc = bacc.Bacc("TRN2", target_bir_lowering=False, num_devices=1)
    arrays, args = {}, []
    for name in _INS:
        a = np.ascontiguousarray(inputs[name])
        arrays["in_" + name] = a
        args.append(nc.dram_tensor("in_" + name, a.shape, mybir.dt.from_np(a.dtype), kind="ExternalInput").ap())
    out = nc.dram_tensor("out_rows", (N, D), F32, kind="ExternalOutput").ap()
    gnn_kernel(nc, *args, out)
    r = run_bass_kernel_spmd(nc, [arrays], core_ids=[0])
    return r.results[0]["out_rows"]
```
